# Optimizing a Trainium2 kernel written in Bass

```python
import numpy as np
import jax
import jax.numpy as jnp

def _softmax(x, axis=-1):
    return jax.nn.softmax(x, axis=axis)

def _gelu(x):
    return jax.nn.gelu(x, approximate=True)

def _silu(x):
    return jax.nn.silu(x)

def _sigmoid(x):
    return jax.nn.sigmoid(x)

def _layernorm(x, axis=-1, eps=1e-05):
    m = jnp.mean(x, axis=axis, keepdims=True)
    v = jnp.var(x, axis=axis, keepdims=True)
    return (x - m) / jnp.sqrt(v + eps)

def _scatter_add(tgt, idx, src, axis=0):
    return tgt.at[idx].add(src)

def _segment_sum(src, seg, n):
    return jax.ops.segment_sum(src, seg, n)
kernel_name = 'mk_adj_resnorm_d2_adj_r2_ee4173'

def setup_inputs(seed: int=0):
    np.random.seed(seed)
    _w = jnp.asarray

    def _rec_inputs():
        import jax
        import jax.numpy as jnp
        _gk = jax.random.key(seed)
        x = -0.0002928 + 1 * jax.random.normal(jax.random.fold_in(_gk, 1), (16, 512, 128), jnp.float32)
        _w = (1.0 + jnp.arange(512, dtype=jnp.float32)) ** (-0.5)
        _w = _w / _w.mean()
        _pij = jnp.clip(0.015625 * _w[:, None] * _w[None, :], 0.0, 1.0)
        _a = jax.random.uniform(jax.random.fold_in(_gk, 2), (512, 512)) < _pij
        _a = jnp.logical_or(_a, jnp.swapaxes(_a, -1, -2))
        _a = jnp.logical_or(_a, jnp.eye(512, dtype=bool))
        _af = _a.astype(jnp.float32)
        _af = _af * jax.random.uniform(jax.random.fold_in(_gk, 3), (512, 512), jnp.float32, 0.05, 1)
        adj = _af
        return (x, adj)
    x, adj = _rec_inputs()

    def _L0_gnn_setup():
        import jax, jax.numpy as jnp
        import numpy as np
        B, N, F_IN, F_OUT, K = (16, 1024, 128, 128, 3)

        def _scaled_laplacian(adj):
            n = adj.shape[0]
            A = adj * (1.0 - jnp.eye(n, dtype=adj.dtype))
            deg = A.sum(axis=1)
            safe = jnp.where(deg > 0, deg, 1.0)
            dinv = jnp.where(deg > 0, 1.0 / jnp.sqrt(safe), 0.0)
            return -(dinv[:, None] * A * dinv[None, :])
        key = jax.random.key(seed)
        k1, k2, k3, _ = jax.random.split(key, 4)
        x = jax.random.normal(k1, (B, N, F_IN), dtype=jnp.float32)
        adj = jax.random.uniform(k2, (N, N), dtype=jnp.float32)
        Ws = jax.random.normal(k3, (K, F_IN, F_OUT), dtype=jnp.float32) / np.float32(np.sqrt(F_IN))
        bias = jnp.zeros((F_OUT,), dtype=jnp.float32)
        return {'x': x, 'adj': adj, 'Ws': Ws, 'bias': bias}
    _L0_gnn_all = _L0_gnn_setup()
    _L0_gnn_in = {k: v for k, v in _L0_gnn_all.items() if k in ('Ws', 'bias')}
    del _L0_gnn_all

    def _L1_gnn_setup():
        import jax, jax.numpy as jnp
        import numpy as np
        B, N, D = (32, 512, 128)
        TIME_STEP = 5
        key = jax.random.key(seed)
        ks = jax.random.split(key, 12)
        s2 = 1.0 / np.sqrt(2 * D)
        s1 = 1.0 / np.sqrt(D)
        return {'input': jax.random.normal(ks[0], (B, N, D), jnp.float32), 'in_matrix': jax.random.uniform(ks[1], (N, N), jnp.float32), 'out_matrix': jax.random.uniform(ks[2], (N, N), jnp.float32), 'w3_w': jax.random.normal(ks[3], (D, 2 * D), jnp.float32) * s2, 'w3_b': jnp.zeros((D,), jnp.float32), 'u3_w': jax.random.normal(ks[4], (D, D), jnp.float32) * s1, 'u3_b': jnp.zeros((D,), jnp.float32), 'w4_w': jax.random.normal(ks[5], (D, 2 * D), jnp.float32) * s2, 'w4_b': jnp.zeros((D,), jnp.float32), 'w5_w': jax.random.normal(ks[6], (D, 2 * D), jnp.float32) * s2, 'w5_b': jnp.zeros((D,), jnp.float32), 'u5_w': jax.random.normal(ks[7], (D, D), jnp.float32) * s1, 'u5_b': jnp.zeros((D,), jnp.float32), 'time_step': TIME_STEP}
    _L1_gnn_all = _L1_gnn_setup()
    _L1_gnn_in = {k: v for k, v in _L1_gnn_all.items() if k in ('w3_w', 'w3_b', 'u3_w', 'u3_b', 'w4_w', 'w4_b', 'w5_w', 'w5_b', 'u5_w', 'u5_b')}
    del _L1_gnn_all
    return {'x': x, 'adj': adj, 'L0_gnn_Ws': _L0_gnn_in['Ws'], 'L0_gnn_bias': _L0_gnn_in['bias'], 'L1_gnn_w3_w': _L1_gnn_in['w3_w'], 'L1_gnn_w3_b': _L1_gnn_in['w3_b'], 'L1_gnn_u3_w': _L1_gnn_in['u3_w'], 'L1_gnn_u3_b': _L1_gnn_in['u3_b'], 'L1_gnn_w4_w': _L1_gnn_in['w4_w'], 'L1_gnn_w4_b': _L1_gnn_in['w4_b'], 'L1_gnn_w5_w': _L1_gnn_in['w5_w'], 'L1_gnn_w5_b': _L1_gnn_in['w5_b'], 'L1_gnn_u5_w': _L1_gnn_in['u5_w'], 'L1_gnn_u5_b': _L1_gnn_in['u5_b']}

def reference(x, adj, L0_gnn_Ws, L0_gnn_bias, L1_gnn_w3_w, L1_gnn_w3_b, L1_gnn_u3_w, L1_gnn_u3_b, L1_gnn_w4_w, L1_gnn_w4_b, L1_gnn_w5_w, L1_gnn_w5_b, L1_gnn_u5_w, L1_gnn_u5_b):
    import jax
    import jax.numpy as jnp

    def _L0_gnn_ref(x, adj, Ws, bias):
        import jax, jax.numpy as jnp
        import numpy as np
        B, N, F_IN, F_OUT, K = (16, 1024, 128, 128, 3)

        def _scaled_laplacian(adj):
            n = adj.shape[0]
            A = adj * (1.0 - jnp.eye(n, dtype=adj.dtype))
            deg = A.sum(axis=1)
            safe = jnp.where(deg > 0, deg, 1.0)
            dinv = jnp.where(deg > 0, 1.0 / jnp.sqrt(safe), 0.0)
            return -(dinv[:, None] * A * dinv[None, :])
        L = _scaled_laplacian(adj)
        Tx0 = x
        out = jnp.einsum('bnf,fo->bno', Tx0, Ws[0])
        Tx1 = jnp.einsum('mn,bnf->bmf', L, Tx0)
        out = out + jnp.einsum('bnf,fo->bno', Tx1, Ws[1])
        for k in range(2, K):
            Tx2 = 2.0 * jnp.einsum('mn,bnf->bmf', L, Tx1) - Tx0
            out = out + jnp.einsum('bnf,fo->bno', Tx2, Ws[k])
            Tx0, Tx1 = (Tx1, Tx2)
        return out + bias

    def _L1_gnn_ref(input, in_matrix, out_matrix, w3_w, w3_b, u3_w, u3_b, w4_w, w4_b, w5_w, w5_b, u5_w, u5_b, time_step):
        import jax, jax.numpy as jnp
        import numpy as np
        B, N, D = (32, 512, 128)
        TIME_STEP = 5

        def step(h, _):
            m_in = jnp.einsum('nm,bmd->bnd', in_matrix, h)
            m_out = jnp.einsum('nm,bmd->bnd', out_matrix, h)
            av = jnp.concatenate([m_in, m_out], axis=-1)
            u3 = h @ u3_w.T + u3_b
            z = jax.nn.sigmoid(av @ w3_w.T + w3_b + u3)
            r = jax.nn.sigmoid(av @ w4_w.T + w4_b + u3)
            hv = jnp.tanh(av @ w5_w.T + w5_b + (r * h @ u5_w.T + u5_b))
            h = (1.0 - z) * h + z * hv
            return (h, None)
        h, _ = jax.lax.scan(step, input, None, length=time_step)
        return h
    x = _layernorm(x + _L0_gnn_ref(x, adj, L0_gnn_Ws, L0_gnn_bias), axis=-1)
    x = _layernorm(x + _L1_gnn_ref(x, adj, adj, L1_gnn_w3_w, L1_gnn_w3_b, L1_gnn_u3_w, L1_gnn_u3_b, L1_gnn_w4_w, L1_gnn_w4_b, L1_gnn_w5_w, L1_gnn_w5_b, L1_gnn_u5_w, L1_gnn_u5_b, 5), axis=-1)
    return x

_drawn_inputs = setup_inputs


def setup_inputs(seed=0):
    import zlib

    import numpy as np

    out = dict(_drawn_inputs(seed))
    spreads = {'L0_gnn_bias': (0.0, 0.1),
     'L1_gnn_w3_b': (0.0, 0.1),
     'L1_gnn_u3_b': (0.0, 0.1),
     'L1_gnn_w4_b': (0.0, 0.8),
     'L1_gnn_w5_b': (0.0, 0.1),
     'L1_gnn_u5_b': (0.0, 0.1)}
    factors = {}
    for name, (base, spread) in spreads.items():
        noise = np.random.default_rng([zlib.crc32(name.encode()), seed]).standard_normal(out[name].shape)
        drawn = base * np.exp(spread * noise) if base else spread * noise
        out[name] = jnp.asarray(drawn.astype(out[name].dtype))
    for name, factor in factors.items():
        out[name] = (out[name] * factor).astype(out[name].dtype)
    return out
```

```python
import concourse.bass as bass
from concourse import mybir
from contextlib import ExitStack


def cheb_gated_graph_kernel(nc, xT, adjT, cheb_w, gate_w, gate_u, gate_b, cheb_b, out):
    f32, f32r = mybir.dt.float32, mybir.dt.float32r
    ALU = mybir.AluOpType
    ACT = mybir.ActivationFunctionType

    P = 128
    B, F, N = xT.shape
    NT = N // P
    GB = 4
    NG = B // GB
    STEPS = 5
    ITEMS = STEPS * GB
    EPS = 1e-5
    NCHEB = 3
    SPLITS = ITEMS + 2

    ctx = ExitStack()
    with ctx:
        def sb(name, shape, dt=f32):
            return ctx.enter_context(nc.sbuf_tensor(name, shape, dt))

        def sem(name):
            return ctx.enter_context(nc.semaphore(name))

        adj = sb("adj", [P, NT, N])
        adj_hi = sb("adj_hi", [P, NT, N], f32r)
        adj_lo = sb("adj_lo", [P, NT, N], f32r)
        dia = sb("dia", [P, NT, P])
        dia_hi = sb("dia_hi", [P, NT, P], f32r)
        dia_lo = sb("dia_lo", [P, NT, P], f32r)
        ident = sb("ident", [P, P])
        ones = sb("ones", [P, 2])
        ones_r = sb("ones_r", [P, 2], f32r)
        chw = sb("chw", [P, NCHEB, P])
        cat = sb("cat", [P, NCHEB, P])
        cat_hi = sb("cat_hi", [P, NCHEB, P], f32r)
        cat_lo = sb("cat_lo", [P, NCHEB, P], f32r)
        gw = sb("gw", [P, 3, 2, P])
        gu = sb("gu", [P, 2, P])
        GZ, GR, GV, U3, U5 = range(5)
        gt = sb("gt", [P, 5, P])
        gt_hi = sb("gt_hi", [P, 5, P], f32r)
        gt_lo = sb("gt_lo", [P, 5, P], f32r)
        gb = sb("gb", [P, 5])
        bias = sb("bias", [P, 3])
        chb = sb("chb", [P, P])
        deg = sb("deg", [P, NT])
        pos = sb("pos", [P, NT])
        neg = sb("neg", [P, NT])
        safe = sb("safe", [P, NT])
        root = sb("root", [P, NT])
        mhalf = sb("mhalf", [P, GB])
        eps = sb("eps", [P, GB])
        dinv = sb("dinv", [P, NT])
        ndinv = sb("ndinv", [P, NT])
        ndinv2 = sb("ndinv2", [P, NT])

        xf = sb("xf", [P, GB, N])
        xf_hi = sb("xf_hi", [P, GB, N], f32r)
        xf_lo = sb("xf_lo", [P, GB, N], f32r)
        y2_hi = sb("y2_hi", [P, NT, GB, P], f32r)
        y2_lo = sb("y2_lo", [P, NT, GB, P], f32r)
        xw1 = sb("xw1", [P, NT, GB, P])
        xw0 = sb("xw0", [P, NT, GB, P])
        y1 = sb("y1", [P, 2, GB, P])
        y1_hi = sb("y1_hi", [P, NT, GB, P], f32r)
        y1_lo = sb("y1_lo", [P, NT, GB, P], f32r)
        hx = sb("hx", [P, NT, GB, P])
        st = sb("st", [P, NT, GB, 6])
        mv = sb("mv", [P, NT, GB, 2])
        ve = sb("ve", [P, NT, GB])
        rstd = sb("rstd", [P, NT, GB])

        hT = sb("hT", [P, GB, N])
        hT_hi = sb("hT_hi", [P, GB, N], f32r)
        hT_lo = sb("hT_lo", [P, GB, N], f32r)
        hn_hi = sb("hn_hi", [P, GB, NT, P], f32r)
        hn_lo = sb("hn_lo", [P, GB, NT, P], f32r)
        m_hi = sb("m_hi", [P, 2, N], f32r)
        m_lo = sb("m_lo", [P, 2, N], f32r)
        zs = sb("zs", [P, 2, N])
        rs = sb("rs", [P, 2, N])
        vs = sb("vs", [P, 2, N])
        rh_hi = sb("rh_hi", [P, 2, N], f32r)
        rh_lo = sb("rh_lo", [P, 2, N], f32r)
        yo = sb("yo", [P, 2, NT, P])
        so = sb("so", [P, 2, NT, 6])
        mo = sb("mo", [P, 2, NT, 2])
        vo = sb("vo", [P, 2, NT])
        ro = sb("ro", [P, 2, NT])

        ps = ctx.enter_context(nc.psum_tensor("ps", [P, 8, N], f32))
        T_BANK, V_BANK, Z_BANK, M_BANK = 0, 2, 4, 6

        ld_adj, ld_w, ld_x = sem("ld_adj"), sem("ld_w"), sem("ld_x")
        st_out = [sem("st_out0"), sem("st_out1")]
        consts = sem("consts")
        dia_ok = sem("dia_ok")
        adj_split = sem("adj_split")
        w_chain = sem("w_chain")
        w_ok = sem("w_ok")
        deg_ok = sem("deg_ok")
        safe_ok = sem("safe_ok")
        root_ok = sem("root_ok")
        dinv_ok = sem("dinv_ok")
        xhi_ok = sem("xhi_ok")
        xlo_ok = sem("xlo_ok")
        xw_done = sem("xw_done")
        y2hi_ok = sem("y2hi_ok")
        xw1_ok = sem("xw1_ok")
        y2lo_ok = sem("y2lo_ok")
        xw0_ok = sem("xw0_ok")
        l1_done = sem("l1_done")
        y1_ok = sem("y1_ok")
        y1hi_ok = sem("y1hi_ok")
        y1lo_ok = sem("y1lo_ok")
        l2_done = sem("l2_done")
        x1_ok = sem("x1_ok")
        bn_ok = sem("bn_ok")
        mv_ok = sem("mv_ok")
        ve_ok = sem("ve_ok")
        rstd_ok = sem("rstd_ok")
        hx_ok = sem("hx_ok")
        hxT_done = sem("hxT_done")
        hT_ok = sem("hT_ok")
        hnhi_ok, hnlo_ok = sem("hnhi_ok"), sem("hnlo_ok")
        hThi_ok, hTlo_ok = sem("hThi_ok"), sem("hTlo_ok")
        m_done, z_done, r_done, v_done = sem("m_done"), sem("z_done"), sem("r_done"), sem("v_done")
        t_done = sem("t_done")
        mhi_ok, mlo_ok = sem("mhi_ok"), sem("mlo_ok")
        z_ok, r_ok, v_ok = sem("z_ok"), sem("r_ok"), sem("v_ok")
        rh_ok, rhhi_ok, rhlo_ok = sem("rh_ok"), sem("rhhi_ok"), sem("rhlo_ok")
        dif_ok, upd_ok, h_ok = sem("dif_ok"), sem("upd_ok"), sem("h_ok")
        yo_ok, bo_ok, mo_ok, out_ok = sem("yo_ok"), sem("bo_ok"), sem("mo_ok"), sem("out_ok")
        vo_ok, ro_ok = sem("vo_ok"), sem("ro_ok")

        block = ctx.enter_context(nc.Block())

        def lap(kt, nt):
            if kt == nt:
                return dia_hi[:, kt, :], dia_lo[:, kt, :]
            cols = slice(nt * P, (nt + 1) * P)
            return adj_hi[:, kt, cols], adj_lo[:, kt, cols]

        @block.sync
        def _(sp):
            sp.dma_start(adj[:], adjT.rearrange("(t p) n -> p t n", p=P)).then_inc(ld_adj, 16)
            out_g = out.rearrange("(g j) (t p) d -> g j p t d", j=GB, p=P)
            xT_g = xT.rearrange("(g b) f n -> g f b n", b=GB)
            with sp.Fori(0, NG) as g:
                sp.dma_start(xf[:], xT_g[bass.ds(g, 1)].rearrange("o f b n -> f (o b) n")).then_inc(ld_x, 16)
                for j in range(GB):
                    sp.wait_ge(out_ok, GB * g + j + 1)
                    if j == GB - 1:
                        sp.wait_ge(xhi_ok, GB * g + GB)
                        sp.wait_ge(xlo_ok, GB * g + GB)
                    sp.dma_start(out_g[bass.ds(g, 1), j].rearrange("o p t d -> p (o t) d"),
                                 yo[:, j % 2]).then_inc(st_out[j % 2], 16)
            for half in st_out:
                sp.wait_ge(half, 16 * (B // 2))

        @block.gpsimd
        def _(pool):
            gp = nc.gpsimd
            gp.memset(ones[:], 1.0).then_inc(consts, 1)
            gp.memset(mhalf[:], -0.5).then_inc(consts, 1)
            gp.memset(eps[:], EPS).then_inc(consts, 1)
            gp.memset(ident[:], 0.0).then_inc(consts, 1)
            pool.wait_ge(consts, 4)
            gp.affine_select(out=ident[:], in_=ident[:], compare_op=ALU.not_equal, fill=1.0, base=0,
                             pattern=[[-1, P]], channel_multiplier=1).then_inc(consts, 1)
            pool.wait_ge(ld_adj, 16)
            for kt in range(NT):
                gp.affine_select(out=dia[:, kt, :], in_=adj[:, kt, kt * P:(kt + 1) * P],
                                 compare_op=ALU.not_equal, fill=0.0, base=0,
                                 pattern=[[-1, P]], channel_multiplier=1).then_inc(dia_ok, 1)
            pool.wait_ge(safe_ok, 1)
            gp.tensor_tensor(root[:], safe[:], mhalf[:, 0:NT], ALU.pow).then_inc(root_ok, 1)

            def state_lo(split, j):
                pool.wait_ge(hThi_ok, split + 1)
                gp.tensor_tensor(hT_lo[:, j], hT[:, j], hT_hi[:, j].bitcast(f32), ALU.subtract).then_inc(hTlo_ok, 1)

            with pool.Fori(0, NG) as g:
                for nt in range(NT):
                    pool.wait_ge(mv_ok, NT * g + nt + 1)
                    gp.tensor_tensor(ve[:, nt, :], mv[:, nt, :, 1], eps[:], ALU.add).then_inc(ve_ok, 1)
                    pool.wait_ge(ve_ok, NT * g + nt + 1)
                    gp.tensor_tensor(rstd[:, nt, :], ve[:, nt, :], mhalf[:, 0:GB], ALU.pow).then_inc(rstd_ok, 1)
                for j in range(GB):
                    state_lo(SPLITS * g + j, j)
                for j in range(2):
                    state_lo(SPLITS * g + GB + j, j)
                with pool.Fori(1, STEPS) as s:
                    for j in range(GB):
                        k = (j + 2) % GB
                        state_lo(SPLITS * g + GB * s + j + 2, k)
                for j in range(GB):
                    pool.wait_ge(mo_ok, GB * g + j + 1)
                    gp.tensor_tensor(vo[:, j % 2, :], mo[:, j % 2, :, 1], eps[:], ALU.add).then_inc(vo_ok, 1)
                    pool.wait_ge(vo_ok, GB * g + j + 1)
                    gp.tensor_tensor(ro[:, j % 2, :], vo[:, j % 2, :], mhalf[:, 0:NT], ALU.pow).then_inc(ro_ok, 1)

        @block.scalar
        def _(act):
            sc = nc.scalar
            act.dma_start(chw[:], cheb_w).then_inc(ld_w, 16)
            act.dma_start(gw[:], gate_w).then_inc(ld_w, 16)
            act.dma_start(gu[:], gate_u).then_inc(ld_w, 16)
            act.dma_start(gb[:], gate_b).then_inc(ld_w, 16)
            act.dma_start(chb[:], cheb_b.partition_broadcast(P)).then_inc(ld_w, 16)
            act.wait_ge(w_ok, 1)
            act.wait_ge(dinv_ok, 1)

            def node_hi(g, n, j, src):
                sc.copy(hn_hi[:, j], src).then_inc(hnhi_ok, 1)

            def candidate(g, n, j):
                act.wait_ge(v_done, ITEMS * g + n + 1)
                sc.activation(vs[:, j % 2], ps[:, V_BANK + j % 2], ACT.Tanh, bias=bias[:, 2:3]).then_inc(v_ok, 1)

            def gate_z(g, n, j, reuse):
                act.wait_ge(z_done, ITEMS * g + n + 1)
                if reuse:
                    act.wait_ge(h_ok, ITEMS * g + n - 1)
                sc.activation(zs[:, j % 2], ps[:, Z_BANK + j % 2], ACT.Sigmoid, bias=bias[:, 0:1]).then_inc(z_ok, 1)

            def gate_r(g, n, j):
                act.wait_ge(r_done, ITEMS * g + n + 1)
                sc.activation(rs[:, j % 2], ps[:, Z_BANK + j % 2], ACT.Sigmoid, bias=bias[:, 1:2]).then_inc(r_ok, 1)

            def state_hi(g, n, j):
                act.wait_ge(h_ok, ITEMS * g + n + 1)
                sc.copy(hT_hi[:, j], hT[:, j]).then_inc(hThi_ok, 1)

            def neighbours_hi(g, n, j):
                act.wait_ge(m_done, ITEMS * g + n + 1)
                sc.copy(m_hi[:, j % 2], ps[:, M_BANK + j % 2]).then_inc(mhi_ok, 1)

            def slot(g, n, j, first, lag1=True, lag2=True):
                a, b = (j - 1) % GB, (j - 2) % GB
                if not first:
                    act.wait_ge(t_done, ITEMS * g + n - GB + 1)
                    node_hi(g, n, j, ps[:, T_BANK + j % 2].rearrange("p (t d) -> p t d", d=P))
                if lag2:
                    candidate(g, n - 2, b)
                if lag1:
                    gate_z(g, n - 1, a, reuse=not (first and j <= 2))
                    gate_r(g, n - 1, a)
                if lag2:
                    state_hi(g, n - 2, b)
                neighbours_hi(g, n, j)

            with act.Fori(0, NG) as g:
                act.wait_ge(ld_x, 16 * g + 16)
                for b in range(GB):
                    sc.copy(xf_hi[:, b], xf[:, b]).then_inc(xhi_ok, 1)
                for nt in range(NT):
                    act.wait_ge(xw_done, NT * g + nt + 1)
                    half = ps[:, 4 * (nt % 2):4 * (nt % 2) + GB]
                    sc.activation(y2_hi[:, nt], half[:, :, 0:P], ACT.Copy, scale=dinv[:, nt:nt + 1]).then_inc(y2hi_ok, 1)
                    sc.activation(xw1[:, nt], half[:, :, P:2 * P], ACT.Copy, scale=dinv[:, nt:nt + 1]).then_inc(xw1_ok, 1)
                for nt in range(NT):
                    act.wait_ge(y1_ok, NT * g + nt + 1)
                    sc.copy(y1_hi[:, nt], y1[:, nt % 2]).then_inc(y1hi_ok, 1)
                act.wait_ge(hx_ok, NT * g + NT)
                for j in range(GB):
                    node_hi(g, j, j, hx[:, :, j, :])
                    act.wait_ge(hxT_done, GB * g + j + 1)
                    sc.copy(hT[:, j], ps[:, j]).then_inc(hT_ok, 1)
                    sc.copy(hT_hi[:, j], ps[:, j]).then_inc(hThi_ok, 1)
                for j in range(GB):
                    slot(g, j, j, first=True, lag1=j >= 1, lag2=j >= 2)
                with act.Fori(1, STEPS) as s:
                    for j in range(GB):
                        slot(g, GB * s + j, j, first=False)
                candidate(g, ITEMS - 2, GB - 2)
                gate_z(g, ITEMS - 1, GB - 1, reuse=True)
                gate_r(g, ITEMS - 1, GB - 1)
                candidate(g, ITEMS - 1, GB - 1)

        @block.vector
        def _(dve):
            ve_ = nc.vector
            chained = [0]

            def link(ins):
                chained[0] += 1
                ins.then_inc(w_chain, 1)
                dve.wait_ge(w_chain, chained[0])

            def less_hi(dst, x, hi):
                return ve_.tensor_tensor(dst, x, hi.bitcast(f32), ALU.subtract)

            dve.wait_ge(ld_adj, 16)
            for kt in range(NT):
                link(ve_.tensor_copy(adj_hi[:, kt], adj[:, kt]))
                less_hi(adj_lo[:, kt], adj[:, kt], adj_hi[:, kt]).then_inc(adj_split, 1)
            dve.wait_ge(dia_ok, NT)
            link(ve_.tensor_copy(dia_hi[:], dia[:]))
            less_hi(dia_lo[:], dia[:], dia_hi[:]).then_inc(adj_split, 1)
            dve.wait_ge(consts, 5)
            ve_.tensor_copy(ones_r[:], ones[:]).then_inc(adj_split, 1)
            dve.wait_ge(ld_w, 16 * 5)
            ve_.tensor_scalar(cat[:, 0], chw[:, 2], 2.0, None, ALU.mult)
            ve_.tensor_copy(cat[:, 1], chw[:, 1])
            link(ve_.tensor_tensor(cat[:, 2], chw[:, 0], chw[:, 2], ALU.subtract))
            link(ve_.tensor_tensor(cat[:, 2], cat[:, 2], ident[:], ALU.add))
            link(ve_.tensor_copy(cat_hi[:], cat[:]))
            less_hi(cat_lo[:], cat[:], cat_hi[:])
            link(ve_.tensor_tensor(gt[:, GZ:GV + 1], gw[:, :, 0], gw[:, :, 1], ALU.add))
            link(ve_.tensor_tensor(gt[:, GR], gt[:, GR], gt[:, GZ], ALU.subtract))
            link(ve_.tensor_copy(gt[:, U3:U5 + 1], gu[:]))
            link(ve_.tensor_copy(gt_hi[:], gt[:]))
            less_hi(gt_lo[:], gt[:], gt_hi[:])
            ve_.tensor_tensor(bias[:, 0:1], gb[:, 0:1], gb[:, 3:4], ALU.add)
            ve_.tensor_tensor(bias[:, 1:2], gb[:, 1:2], gb[:, 3:4], ALU.add)
            ve_.tensor_tensor(bias[:, 2:3], gb[:, 2:3], gb[:, 4:5], ALU.add).then_inc(w_ok, 1)
            dve.wait_ge(deg_ok, 1)
            link(ve_.tensor_copy(deg[:], ps[:, 0, 0:2 * NT].rearrange("p (t two) -> p t two", two=2)[:, :, 0]))
            link(ve_.tensor_scalar(pos[:], deg[:], 0.0, None, ALU.is_gt))
            link(ve_.tensor_scalar(neg[:], pos[:], -1.0, 1.0, ALU.mult, ALU.add))
            link(ve_.tensor_tensor(safe[:], deg[:], pos[:], ALU.mult))
            ve_.tensor_tensor(safe[:], safe[:], neg[:], ALU.add).then_inc(safe_ok, 1)
            dve.wait_ge(root_ok, 1)
            link(ve_.tensor_tensor(dinv[:], root[:], pos[:], ALU.mult))
            link(ve_.tensor_scalar(ndinv[:], dinv[:], -1.0, None, ALU.mult))
            ve_.tensor_tensor(ndinv2[:], ndinv[:], dinv[:], ALU.mult).then_inc(dinv_ok, 1)
            dve.wait_ge(dinv_ok, 1)

            def neighbours_lo(g, n, j):
                dve.wait_ge(mhi_ok, ITEMS * g + n + 1)
                less_hi(m_lo[:, j % 2], ps[:, M_BANK + j % 2], m_hi[:, j % 2]).then_inc(mlo_ok, 1)

            def node_lo(g, n, j, src):
                dve.wait_ge(hnhi_ok, ITEMS * g + n + 1)
                less_hi(hn_lo[:, j], src, hn_hi[:, j]).then_inc(hnlo_ok, 1)

            def update(g, n, j):
                dve.wait_ge(v_ok, ITEMS * g + n + 1)
                ve_.tensor_tensor(vs[:, j % 2], vs[:, j % 2], hT[:, j], ALU.subtract).then_inc(dif_ok, 1)
                dve.wait_ge(dif_ok, ITEMS * g + n + 1)
                ve_.tensor_tensor(vs[:, j % 2], vs[:, j % 2], zs[:, j % 2], ALU.mult).then_inc(upd_ok, 1)
                dve.wait_ge(upd_ok, ITEMS * g + n + 1)
                ve_.tensor_tensor(hT[:, j], hT[:, j], vs[:, j % 2], ALU.add).then_inc(h_ok, 1)

            def reset(g, n, j):
                dve.wait_ge(r_ok, ITEMS * g + n + 1)
                ve_.tensor_tensor(rs[:, j % 2], rs[:, j % 2], hT[:, j], ALU.mult).then_inc(rh_ok, 1)
                dve.wait_ge(rh_ok, ITEMS * g + n + 1)
                ve_.tensor_copy(rh_hi[:, j % 2], rs[:, j % 2]).then_inc(rhhi_ok, 1)
                dve.wait_ge(rhhi_ok, ITEMS * g + n + 1)
                less_hi(rh_lo[:, j % 2], rs[:, j % 2], rh_hi[:, j % 2]).then_inc(rhlo_ok, 1)

            def slot(g, n, j, first, lag1=True, lag2=True):
                a, b = (j - 1) % GB, (j - 2) % GB
                if lag1:
                    neighbours_lo(g, n - 1, a)
                if not first:
                    node_lo(g, n, j, ps[:, T_BANK + j % 2].rearrange("p (t d) -> p t d", d=P))
                if lag2:
                    update(g, n - 2, b)
                if lag1:
                    reset(g, n - 1, a)

            def normalize(g, nt):
                dve.wait_ge(rstd_ok, NT * g + nt + 1)
                for b in range(GB):
                    last = ve_.tensor_scalar(hx[:, nt, b, :], hx[:, nt, b, :], mv[:, nt, b, 0:1],
                                             rstd[:, nt, b:b + 1], ALU.subtract, ALU.mult)
                last.then_inc(hx_ok, 1)

            with dve.Fori(0, NG) as g:
                for b in range(GB):
                    dve.wait_ge(xhi_ok, GB * g + b + 1)
                    less_hi(xf_lo[:, b], xf[:, b], xf_hi[:, b]).then_inc(xlo_ok, 1)
                for nt in range(NT):
                    dve.wait_ge(xw1_ok, NT * g + nt + 1)
                    half = ps[:, 4 * (nt % 2):4 * (nt % 2) + GB]
                    ve_.scalar_tensor_tensor(y2_lo[:, nt], half[:, :, 0:P], dinv[:, nt:nt + 1],
                                             y2_hi[:, nt].bitcast(f32), ALU.mult, ALU.subtract).then_inc(y2lo_ok, 1)
                    ve_.tensor_tensor(xw0[:, nt], half[:, :, 2 * P:3 * P],
                                      chb[:].unsqueeze(1).broadcast_to([P, GB, P]), ALU.add).then_inc(xw0_ok, 1)
                for nt in range(NT):
                    dve.wait_ge(l1_done, NT * g + nt + 1)
                    if nt >= 2:
                        dve.wait_ge(y1hi_ok, NT * g + nt - 1)
                    ve_.scalar_tensor_tensor(y1[:, nt % 2], ps[:, nt].rearrange("p (b d) -> p b d", d=P),
                                             ndinv2[:, nt:nt + 1], xw1[:, nt], ALU.mult, ALU.add).then_inc(y1_ok, 1)
                    dve.wait_ge(y1hi_ok, NT * g + nt + 1)
                    less_hi(y1_lo[:, nt], y1[:, nt % 2], y1_hi[:, nt]).then_inc(y1lo_ok, 1)
                for nt in range(NT):
                    dve.wait_ge(l2_done, NT * g + nt + 1)
                    dve.wait_ge(xw0_ok, NT * g + nt + 1)
                    ve_.scalar_tensor_tensor(hx[:, nt], ps[:, 4 + nt].rearrange("p (b d) -> p b d", d=P),
                                             ndinv[:, nt:nt + 1], xw0[:, nt], ALU.mult, ALU.add).then_inc(x1_ok, 1)
                    dve.wait_ge(x1_ok, NT * g + nt + 1)
                    for b in range(GB):
                        last = ve_.bn_stats(st[:, nt, b, :], hx[:, nt, b, :])
                    last.then_inc(bn_ok, 1)
                    dve.drain()
                    for b in range(GB):
                        last = ve_.bn_aggr(mv[:, nt, b, :], st[:, nt, b, :])
                    last.then_inc(mv_ok, 1)
                    if nt >= 1:
                        normalize(g, nt - 1)
                normalize(g, NT - 1)
                for j in range(GB):
                    node_lo(g, j, j, hx[:, :, j, :])
                for j in range(GB):
                    slot(g, j, j, first=True, lag1=j >= 1, lag2=j >= 2)
                with dve.Fori(1, STEPS) as s:
                    for j in range(GB):
                        slot(g, GB * s + j, j, first=False)
                neighbours_lo(g, ITEMS - 1, GB - 1)
                update(g, ITEMS - 2, GB - 2)
                reset(g, ITEMS - 1, GB - 1)
                update(g, ITEMS - 1, GB - 1)
                for j in range(GB):
                    dve.wait_ge(t_done, ITEMS * g + ITEMS - GB + j + 1)
                    if j >= 2:
                        dve.wait_ge(st_out[j % 2], 16 * (GB // 2 * g + j // 2))
                    ve_.tensor_tensor(yo[:, j % 2], ps[:, T_BANK + j % 2].rearrange("p (t d) -> p t d", d=P),
                                      hx[:, :, j, :], ALU.add).then_inc(yo_ok, 1)
                    dve.wait_ge(yo_ok, GB * g + j + 1)
                    for t in range(NT):
                        last = ve_.bn_stats(so[:, j % 2, t, :], yo[:, j % 2, t, :])
                    last.then_inc(bo_ok, 1)
                    dve.drain()
                    for t in range(NT):
                        last = ve_.bn_aggr(mo[:, j % 2, t, :], so[:, j % 2, t, :])
                    last.then_inc(mo_ok, 1)
                    dve.wait_ge(ro_ok, GB * g + j + 1)
                    for t in range(NT):
                        last = ve_.tensor_scalar(yo[:, j % 2, t, :], yo[:, j % 2, t, :], mo[:, j % 2, t, 0:1],
                                                 ro[:, j % 2, t:t + 1], ALU.subtract, ALU.mult)
                    last.then_inc(out_ok, 1)
                for half in st_out:
                    dve.wait_ge(half, 16 * (GB // 2 * g + GB // 2))

        @block.tensor
        def _(pe):
            mm = nc.tensor.matmul
            pe.wait_ge(adj_split, NT + 2)
            for nt in range(NT):
                for kt in range(NT):
                    hi, lo = lap(kt, nt)
                    mm(ps[:, 0, 2 * nt:2 * nt + 2], hi, ones_r[:], start=kt == 0, stop=False)
                    last = mm(ps[:, 0, 2 * nt:2 * nt + 2], lo, ones_r[:], start=False, stop=kt == NT - 1)
            last.then_inc(deg_ok, 1)
            pe.wait_ge(w_ok, 1)
            pe.wait_ge(dinv_ok, 1)

            def weight(w, bank, hi, lo, start, stop):
                mm(bank, gt_hi[:, w], hi, start=start, stop=False)
                mm(bank, gt_lo[:, w], hi, start=False, stop=False)
                return mm(bank, gt_hi[:, w], lo, start=False, stop=stop)

            def neighbours(g, n, j, part):
                bank = ps[:, M_BANK + j % 2]
                runs = [(hn_hi, kt, a) for kt in range(NT) for a in (adj_hi, adj_lo)]
                runs += [(hn_lo, kt, adj_hi) for kt in range(NT)]
                half = len(runs) // 2
                for i in range(part * half, (part + 1) * half):
                    h, kt, a = runs[i]
                    if i == 0:
                        pe.wait_ge(hnhi_ok, ITEMS * g + n + 1)
                    if i == 2 * NT:
                        pe.wait_ge(hnlo_ok, ITEMS * g + n + 1)
                    last = mm(bank, h[:, j, kt, :], a[:, kt], start=i == 0, stop=i == len(runs) - 1)
                if part == 1:
                    last.then_inc(m_done, 1)

            def gates_z(g, n, j):
                a = j % 2
                pe.wait_ge(hTlo_ok, SPLITS * g + n + 1)
                weight(U3, ps[:, Z_BANK + a], hT_hi[:, j], hT_lo[:, j], True, False)
                pe.wait_ge(mlo_ok, ITEMS * g + n + 1)
                weight(GZ, ps[:, Z_BANK + a], m_hi[:, a], m_lo[:, a], False, True).then_inc(z_done, 1)

            def gates_r(g, n, j):
                a = j % 2
                bank = ps[:, Z_BANK + a]
                pe.wait_ge(z_ok, ITEMS * g + n + 1)
                for i, (w, m) in enumerate(((gt_hi, m_hi), (gt_lo, m_hi), (gt_hi, m_lo))):
                    last = mm(bank, w[:, GR], m[:, a], start=False, stop=i == 2, skip_group_check=True)
                last.then_inc(r_done, 1)

            def cand_m(g, n, j, reuse):
                a = j % 2
                if reuse:
                    pe.wait_ge(v_ok, ITEMS * g + n - 1)
                weight(GV, ps[:, V_BANK + a], m_hi[:, a], m_lo[:, a], True, False)

            def cand_h(g, n, j):
                a = j % 2
                bank = ps[:, V_BANK + a]
                pe.wait_ge(rhhi_ok, ITEMS * g + n + 1)
                mm(bank, gt_hi[:, U5], rh_hi[:, a], start=False, stop=False)
                mm(bank, gt_lo[:, U5], rh_hi[:, a], start=False, stop=False)
                pe.wait_ge(rhlo_ok, ITEMS * g + n + 1)
                mm(bank, gt_hi[:, U5], rh_lo[:, a], start=False, stop=True).then_inc(v_done, 1)

            def to_node(g, n, j):
                pe.wait_ge(h_ok, ITEMS * g + n + 1)
                for t in range(NT):
                    last = nc.tensor.transpose(ps[:, T_BANK + j % 2, t * P:(t + 1) * P],
                                               hT[:, j, t * P:(t + 1) * P], ident[:])
                last.then_inc(t_done, 1)

            def slot(g, n, j, first, lag1=True, lag2=True):
                a = (j - 1) % GB
                if not first:
                    pe.wait_ge(hnlo_ok, ITEMS * g + n - 1)
                    to_node(g, n - GB, j)
                if lag2:
                    cand_h(g, n - 2, (j - 2) % GB)
                if lag1:
                    gates_z(g, n - 1, a)
                neighbours(g, n, j, 0)
                if lag1:
                    gates_r(g, n - 1, a)
                    cand_m(g, n - 1, a, reuse=not (first and j <= 2))
                neighbours(g, n, j, 1)

            with pe.Fori(0, NG) as g:
                pe.wait_ge(xlo_ok, GB * g + GB)
                for nt in range(NT):
                    if nt >= 2:
                        pe.wait_ge(xw0_ok, NT * g + nt - 1)
                    for b in range(GB):
                        bank = ps[:, 4 * (nt % 2) + b, 0:NCHEB * P]
                        rows = slice(nt * P, (nt + 1) * P)
                        mm(bank, xf_hi[:, b, rows], cat_hi[:].rearrange("p k d -> p (k d)"), start=True, stop=False)
                        mm(bank, xf_hi[:, b, rows], cat_lo[:].rearrange("p k d -> p (k d)"), start=False, stop=False)
                        last = mm(bank, xf_lo[:, b, rows], cat_hi[:].rearrange("p k d -> p (k d)"), start=False, stop=True)
                    last.then_inc(xw_done, 1)

                def aggregate(bank, nt, hi, lo):
                    flat = "p b d -> p (b d)"
                    for kt in range(NT):
                        a_hi, a_lo = lap(kt, nt)
                        mm(bank, a_hi, hi[:, kt].rearrange(flat), start=kt == 0, stop=False)
                        mm(bank, a_lo, hi[:, kt].rearrange(flat), start=False, stop=False)
                        last = mm(bank, a_hi, lo[:, kt].rearrange(flat), start=False, stop=kt == NT - 1)
                    return last

                pe.wait_ge(xw0_ok, NT * g + NT)
                for nt in range(NT):
                    aggregate(ps[:, nt], nt, y2_hi, y2_lo).then_inc(l1_done, 1)
                pe.wait_ge(y1lo_ok, NT * g + NT)
                for nt in range(NT):
                    aggregate(ps[:, 4 + nt], nt, y1_hi, y1_lo).then_inc(l2_done, 1)
                pe.wait_ge(hx_ok, NT * g + NT)
                for j in range(GB):
                    for t in range(NT):
                        last = nc.tensor.transpose(ps[:, j, t * P:(t + 1) * P], hx[:, t, j, :], ident[:])
                    last.then_inc(hxT_done, 1)
                for j in range(GB):
                    slot(g, j, j, first=True, lag1=j >= 1, lag2=j >= 2)
                with pe.Fori(1, STEPS) as s:
                    for j in range(GB):
                        slot(g, GB * s + j, j, first=False)
                cand_h(g, ITEMS - 2, GB - 2)
                gates_z(g, ITEMS - 1, GB - 1)
                gates_r(g, ITEMS - 1, GB - 1)
                cand_m(g, ITEMS - 1, GB - 1, reuse=True)
                cand_h(g, ITEMS - 1, GB - 1)
                for j in range(GB):
                    if j < 2:
                        pe.wait_ge(hnlo_ok, ITEMS * g + ITEMS)
                    else:
                        pe.wait_ge(yo_ok, GB * g + j - 1)
                    to_node(g, ITEMS - GB + j, j)
                pe.wait_ge(yo_ok, GB * g + GB)


def kernel(**inputs):
    import numpy as np
    import concourse.bacc as bacc
    from concourse.bass_utils import run_bass_kernel_spmd

    def arr(name):
        return np.asarray(inputs[name])

    P = 128
    x = arr("x")
    xT = np.ascontiguousarray(x.transpose(0, 2, 1))
    adjT = np.ascontiguousarray(arr("adj").T)
    cheb_w = np.ascontiguousarray(arr("L0_gnn_Ws").transpose(1, 0, 2))
    gate_w = np.ascontiguousarray(np.stack([arr(f"L1_gnn_w{k}_w").T.reshape(2, P, P) for k in (3, 4, 5)])
                                  .transpose(2, 0, 1, 3))
    gate_u = np.ascontiguousarray(np.stack([arr(f"L1_gnn_u{k}_w").T for k in (3, 5)]).transpose(1, 0, 2))
    gate_b = np.ascontiguousarray(np.stack([arr(f"L1_gnn_{k}_b") for k in ("w3", "w4", "w5", "u3", "u5")]).T)
    cheb_b = arr("L0_gnn_bias")
    arrays = {"xT": xT, "adjT": adjT, "cheb_w": cheb_w, "gate_w": gate_w, "gate_u": gate_u,
              "gate_b": gate_b, "cheb_b": cheb_b}

    nc = bacc.Bacc("TRN2", target_bir_lowering=False, num_devices=1)
    args = [nc.dram_tensor(f"in_{n}", a.shape, mybir.dt.from_np(a.dtype), kind="ExternalInput").ap()
            for n, a in arrays.items()]
    out = nc.dram_tensor("out_0", x.shape, mybir.dt.float32, kind="ExternalOutput").ap()
    cheb_gated_graph_kernel(nc, *args, out)
    r = run_bass_kernel_spmd(nc, [{f"in_{n}": a for n, a in arrays.items()}], core_ids=[0])
    return r.results[0]["out_0"]
```

```python
import concourse.bass as bass
from concourse import mybir
from contextlib import ExitStack


def cheb_gated_graph_kernel(nc, xT, adjT, cheb_w, gate_w, gate_u, gate_b, cheb_b, out):
    f32, f32r = mybir.dt.float32, mybir.dt.float32r
    ALU = mybir.AluOpType
    ACT = mybir.ActivationFunctionType

    P = 128
    B, F, N = xT.shape
    NT = N // P
    GB = 4
    NG = B // GB
    STEPS = 5
    ITEMS = STEPS * GB
    EPS = 1e-5
    NCHEB = 3
    SPLITS = ITEMS + 2

    ctx = ExitStack()
    with ctx:
        def sb(name, shape, dt=f32):
            return ctx.enter_context(nc.sbuf_tensor(name, shape, dt))

        def sem(name):
            return ctx.enter_context(nc.semaphore(name))

        adj = sb("adj", [P, NT, N])
        adj_hi = sb("adj_hi", [P, NT, N], f32r)
        adj_lo = sb("adj_lo", [P, NT, N], f32r)
        dia = sb("dia", [P, NT, P])
        dia_hi = sb("dia_hi", [P, NT, P], f32r)
        dia_lo = sb("dia_lo", [P, NT, P], f32r)
        ident = sb("ident", [P, P])
        ones = sb("ones", [P, 2])
        ones_r = sb("ones_r", [P, 2], f32r)
        chw = sb("chw", [P, NCHEB, P])
        cat = sb("cat", [P, NCHEB, P])
        cat_hi = sb("cat_hi", [P, NCHEB, P], f32r)
        cat_lo = sb("cat_lo", [P, NCHEB, P], f32r)
        gw = sb("gw", [P, 3, 2, P])
        gu = sb("gu", [P, 2, P])
        GZ, GR, GV, U3, U5 = range(5)
        gt = sb("gt", [P, 5, P])
        gt_hi = sb("gt_hi", [P, 5, P], f32r)
        gt_lo = sb("gt_lo", [P, 5, P], f32r)
        gb = sb("gb", [P, 5])
        bias = sb("bias", [P, 3])
        chb = sb("chb", [P, P])
        deg = sb("deg", [P, NT])
        pos = sb("pos", [P, NT])
        neg = sb("neg", [P, NT])
        safe = sb("safe", [P, NT])
        zero = sb("zero", [P, GB])
        root = sb("root", [P, NT])
        mhalf = sb("mhalf", [P, GB])
        eps = sb("eps", [P, GB])
        dinv = sb("dinv", [P, NT])
        ndinv = sb("ndinv", [P, NT])
        ndinv2 = sb("ndinv2", [P, NT])

        xf = sb("xf", [P, GB, N])
        xf_hi = sb("xf_hi", [P, GB, N], f32r)
        xf_lo = sb("xf_lo", [P, GB, N], f32r)
        y2_hi = sb("y2_hi", [P, NT, GB, P], f32r)
        y2_lo = sb("y2_lo", [P, NT, GB, P], f32r)
        xw1 = sb("xw1", [P, NT, GB, P])
        xw0 = sb("xw0", [P, NT, GB, P])
        y1_hi = sb("y1_hi", [P, NT, GB, P], f32r)
        y1_lo = sb("y1_lo", [P, NT, GB, P], f32r)
        hx = sb("hx", [P, NT, GB, P])
        st = sb("st", [P, NT, GB, 6])
        mv = sb("mv", [P, NT, GB, 2])
        ve = sb("ve", [P, NT, GB])
        rstd = sb("rstd", [P, NT, GB])
        mr = sb("mr", [P, NT, GB])
        nmr = sb("nmr", [P, NT, GB])

        hT = sb("hT", [P, GB, N])
        hT_hi = sb("hT_hi", [P, GB, N], f32r)
        hT_lo = sb("hT_lo", [P, GB, N], f32r)
        hn_hi = sb("hn_hi", [P, GB, NT, P], f32r)
        hn_lo = sb("hn_lo", [P, GB, NT, P], f32r)
        m_hi = sb("m_hi", [P, 2, N], f32r)
        m_lo = sb("m_lo", [P, 2, N], f32r)
        zs = sb("zs", [P, 2, N])
        rs = sb("rs", [P, 2, N])
        vs = sb("vs", [P, 2, N])
        rh_hi = sb("rh_hi", [P, 2, N], f32r)
        rh_lo = sb("rh_lo", [P, 2, N], f32r)
        yo = sb("yo", [P, 2, NT, P])
        so = sb("so", [P, 2, NT, 6])
        mo = sb("mo", [P, 2, NT, 2])
        vo = sb("vo", [P, 2, NT])
        ro = sb("ro", [P, 2, NT])
        mro = sb("mro", [P, 2, NT])
        nmro = sb("nmro", [P, 2, NT])

        ps = ctx.enter_context(nc.psum_tensor("ps", [P, 8, N], f32))
        T_BANK, V_BANK, Z_BANK, M_BANK = 0, 2, 4, 6
        UNITS = NT * GB // 2
        X_BANKS = (M_BANK, Z_BANK, V_BANK)
        L1_BANK, L2_BANK = 2, 0

        ld_adj, ld_w, ld_x = sem("ld_adj"), sem("ld_w"), sem("ld_x")
        st_out = [sem("st_out0"), sem("st_out1")]
        consts = sem("consts")
        dia_ok = sem("dia_ok")
        adjhi_ok = sem("adjhi_ok")
        adj_split = sem("adj_split")
        w_chain = sem("w_chain")
        cat_ok = sem("cat_ok")
        w_ok = sem("w_ok")
        deg_ok = sem("deg_ok")
        safe_ok = sem("safe_ok")
        root_ok = sem("root_ok")
        dinv_ok = sem("dinv_ok")
        xhi_ok = sem("xhi_ok")
        xlo_ok = sem("xlo_ok")
        xw_done = sem("xw_done")
        xw1_ok = sem("xw1_ok")
        xw0_ok = sem("xw0_ok")
        l1_done = sem("l1_done")
        y1_ok = sem("y1_ok")
        y1hi_ok = sem("y1hi_ok")
        y1lo_ok = sem("y1lo_ok")
        l2_done = sem("l2_done")
        x1_ok = sem("x1_ok")
        mv_ok = sem("mv_ok")
        ve_ok = sem("ve_ok")
        rstd_ok = sem("rstd_ok")
        mr_ok = sem("mr_ok")
        nmr_ok = sem("nmr_ok")
        hx_ok = sem("hx_ok")
        hxT_done = sem("hxT_done")
        hnhi_ok, hnlo_ok = sem("hnhi_ok"), sem("hnlo_ok")
        hThi_ok, hTlo_ok = sem("hThi_ok"), sem("hTlo_ok")
        m_done, z_done, r_done, v_done = sem("m_done"), sem("z_done"), sem("r_done"), sem("v_done")
        t_done = sem("t_done")
        mhi_ok, mlo_ok = sem("mhi_ok"), sem("mlo_ok")
        z_ok, r_ok, v_ok = sem("z_ok"), sem("r_ok"), sem("v_ok")
        rh_ok, rhhi_ok, rhlo_ok = sem("rh_ok"), sem("rhhi_ok"), sem("rhlo_ok")
        dif_ok, upd_ok, h_ok = sem("dif_ok"), sem("upd_ok"), sem("h_ok")
        yo_ok, mo_ok = sem("yo_ok"), sem("mo_ok")
        vo_ok, ro_ok, mro_ok, nmro_ok = sem("vo_ok"), sem("ro_ok"), sem("mro_ok"), sem("nmro_ok")
        out_ok = sem("out_ok")

        block = ctx.enter_context(nc.Block())

        def lap(kt, nt):
            if kt == nt:
                return dia_hi[:, kt, :], dia_lo[:, kt, :]
            cols = slice(nt * P, (nt + 1) * P)
            return adj_hi[:, kt, cols], adj_lo[:, kt, cols]

        def unit(u):
            nt, b = u // 2, 2 * (u % 2)
            bank = X_BANKS[u % 3]
            return nt, slice(b, b + 2), ps[:, bank:bank + 2]

        def t_bank(j):
            return ps[:, T_BANK + j % 2].rearrange("p (t d) -> p t d", d=P)

        @block.sync
        def _(sp):
            def load_x(g):
                sp.dma_start(xf[:], xT[GB * g:GB * g + GB].rearrange("b f n -> f b n")).then_inc(ld_x, 16)

            load_x(0)
            sp.dma_start(adj[:], adjT.rearrange("(t p) n -> p t n", p=P)).then_inc(ld_adj, 16)
            for g in range(NG):
                if g + 1 < NG:
                    if g >= 1:
                        for half in st_out:
                            sp.wait_ge(half, 16 * (GB // 2) * g)
                    sp.wait_ge(xhi_ok, GB * g + GB)
                    sp.wait_ge(xlo_ok, GB * g + GB)
                    load_x(g + 1)
                for j in range(GB):
                    sp.wait_ge(out_ok, GB * g + j + 1)
                    sp.dma_start(out[GB * g + j].rearrange("(t p) d -> p t d", p=P),
                                 yo[:, j % 2]).then_inc(st_out[j % 2], 16)
            for half in st_out:
                sp.wait_ge(half, 16 * (B // 2))

        @block.gpsimd
        def _(pool):
            gp = nc.gpsimd
            gp.memset(ones[:], 1.0).then_inc(consts, 1)
            gp.memset(mhalf[:], -0.5).then_inc(consts, 1)
            gp.memset(eps[:], EPS).then_inc(consts, 1)
            gp.memset(zero[:], 0.0).then_inc(consts, 1)
            gp.memset(ident[:], 0.0).then_inc(consts, 1)
            pool.wait_ge(consts, 5)
            gp.affine_select(out=ident[:], in_=ident[:], compare_op=ALU.not_equal, fill=1.0, base=0,
                             pattern=[[-1, P]], channel_multiplier=1).then_inc(consts, 1)
            pool.wait_ge(ld_adj, 16)
            for kt in range(NT):
                gp.affine_select(out=dia[:, kt, :], in_=adj[:, kt, kt * P:(kt + 1) * P],
                                 compare_op=ALU.not_equal, fill=0.0, base=0,
                                 pattern=[[-1, P]], channel_multiplier=1).then_inc(dia_ok, 1)
            pool.wait_ge(safe_ok, 1)
            gp.tensor_tensor(root[:], safe[:], mhalf[:, 0:NT], ALU.pow).then_inc(root_ok, 1)

            def scale_shift(count, var, mean, v, r, m, nm, ready, sems):
                v_sem, r_sem, m_sem, nm_sem = sems
                pool.wait_ge(ready, count)
                gp.tensor_tensor(v, var, eps[:], ALU.add).then_inc(v_sem, 1)
                pool.wait_ge(v_sem, count)
                gp.tensor_tensor(r, v, mhalf[:], ALU.pow).then_inc(r_sem, 1)
                pool.wait_ge(r_sem, count)
                gp.tensor_tensor(m, mean, r, ALU.mult).then_inc(m_sem, 1)
                pool.wait_ge(m_sem, count)
                gp.tensor_tensor(nm, zero[:], m, ALU.subtract).then_inc(nm_sem, 1)

            def first_norm(g):
                for nt in range(NT):
                    scale_shift(NT * g + nt + 1, mv[:, nt, :, 1], mv[:, nt, :, 0], ve[:, nt], rstd[:, nt],
                                mr[:, nt], nmr[:, nt], mv_ok, (ve_ok, rstd_ok, mr_ok, nmr_ok))

            def last_norm(g):
                for j in range(GB):
                    a = j % 2
                    scale_shift(GB * g + j + 1, mo[:, a, :, 1], mo[:, a, :, 0], vo[:, a], ro[:, a],
                                mro[:, a], nmro[:, a], mo_ok, (vo_ok, ro_ok, mro_ok, nmro_ok))

            def state_lo(split, j):
                pool.wait_ge(hThi_ok, split + 1)
                gp.tensor_tensor(hT_lo[:, j], hT[:, j], hT_hi[:, j].bitcast(f32), ALU.subtract).then_inc(hTlo_ok, 1)

            def gated(g, split_next):
                for j in range(GB):
                    state_lo(SPLITS * g + j, j)
                for j in range(2):
                    state_lo(SPLITS * g + GB + j, j)
                    if split_next:
                        for b in (2 * j, 2 * j + 1):
                            pool.wait_ge(xhi_ok, GB * g + GB + b + 1)
                            gp.tensor_tensor(xf_lo[:, b], xf[:, b], xf_hi[:, b].bitcast(f32),
                                             ALU.subtract).then_inc(xlo_ok, 1)
                with pool.Fori(1, STEPS) as s:
                    for j in range(GB):
                        state_lo(SPLITS * g + GB * s + j + 2, (j + 2) % GB)

            first_norm(0)
            with pool.Fori(0, NG - 1) as g:
                gated(g, True)
                last_norm(g)
                first_norm(g + 1)
            gated(NG - 1, False)
            last_norm(NG - 1)

        @block.scalar
        def _(act):
            sc = nc.scalar
            act.dma_start(chw[:], cheb_w).then_inc(ld_w, 16)
            act.dma_start(gw[:], gate_w).then_inc(ld_w, 16)
            act.dma_start(gu[:], gate_u).then_inc(ld_w, 16)
            act.dma_start(gb[:], gate_b).then_inc(ld_w, 16)
            act.dma_start(chb[:], cheb_b.partition_broadcast(P)).then_inc(ld_w, 16)

            def candidate(g, n, j):
                act.wait_ge(v_done, ITEMS * g + n + 1)
                sc.activation(vs[:, j % 2], ps[:, V_BANK + j % 2], ACT.Tanh, bias=bias[:, 2:3]).then_inc(v_ok, 1)

            def gate_z(g, n, j, reuse=True):
                act.wait_ge(z_done, ITEMS * g + n + 1)
                if reuse:
                    act.wait_ge(h_ok, ITEMS * g + n - 1)
                sc.activation(zs[:, j % 2], ps[:, Z_BANK + j % 2], ACT.Sigmoid, bias=bias[:, 0:1]).then_inc(z_ok, 1)

            def gate_r(g, n, j):
                act.wait_ge(r_done, ITEMS * g + n + 1)
                sc.activation(rs[:, j % 2], ps[:, Z_BANK + j % 2], ACT.Sigmoid, bias=bias[:, 1:2]).then_inc(r_ok, 1)

            def state_hi(g, n, j):
                act.wait_ge(h_ok, ITEMS * g + n + 1)
                sc.copy(hT_hi[:, j], hT[:, j]).then_inc(hThi_ok, 1)

            def neighbours_hi(g, n, j):
                act.wait_ge(m_done, ITEMS * g + n + 1)
                sc.copy(m_hi[:, j % 2], ps[:, M_BANK + j % 2]).then_inc(mhi_ok, 1)

            def slot(g, n, j, first, lag2=True):
                a, b = (j - 1) % GB, (j - 2) % GB
                if not first:
                    act.wait_ge(t_done, ITEMS * g + n - GB + 1)
                    sc.copy(hn_hi[:, j], t_bank(j)).then_inc(hnhi_ok, 1)
                if lag2:
                    candidate(g, n - 2, b)
                gate_z(g, n - 1, a, reuse=not (first and j <= 2))
                gate_r(g, n - 1, a)
                if lag2:
                    state_hi(g, n - 2, b)
                neighbours_hi(g, n, j)

            def first_state(g, j):
                act.wait_ge(hxT_done, GB * g + j + 1)
                sc.copy(hT[:, j], ps[:, j])
                sc.copy(hT_hi[:, j], ps[:, j]).then_inc(hThi_ok, 1)

            def split_x(g, b):
                act.wait_ge(ld_x, 16 * g + 16)
                sc.copy(xf_hi[:, b], xf[:, b]).then_inc(xhi_ok, 1)

            def x_unit(g, u):
                nt, bs, banks = unit(u)
                act.wait_ge(xw_done, UNITS * g + u + 1)
                sc.activation(y2_hi[:, nt, bs], banks[:, :, 0:P], ACT.Copy, scale=dinv[:, nt:nt + 1])
                sc.activation(xw1[:, nt, bs], banks[:, :, P:2 * P], ACT.Copy, scale=dinv[:, nt:nt + 1]).then_inc(xw1_ok, 1)

            def last_norm(g, j):
                act.wait_ge(nmro_ok, GB * g + j + 1)
                for t in range(NT):
                    last = sc.activation(yo[:, j % 2, t], yo[:, j % 2, t], ACT.Identity,
                                         scale=ro[:, j % 2, t:t + 1], bias=nmro[:, j % 2, t:t + 1])
                last.then_inc(out_ok, 1)

            def conv_rest(g):
                for nt in range(NT):
                    act.wait_ge(y1_ok, NT * g + nt + 1)
                    sc.copy(y1_hi[:, nt], xw1[:, nt]).then_inc(y1hi_ok, 1)
                for nt in range(NT):
                    act.wait_ge(nmr_ok, NT * g + nt + 1)
                    for b in range(GB):
                        last = sc.activation(hx[:, nt, b], hx[:, nt, b], ACT.Identity,
                                             scale=rstd[:, nt, b:b + 1], bias=nmr[:, nt, b:b + 1])
                    last.then_inc(hx_ok, 1)
                    act.wait_ge(hx_ok, NT * g + nt + 1)
                    sc.copy(hn_hi[:, :, nt], hx[:, nt]).then_inc(hnhi_ok, 1)

            def gated(g, split_next):
                first_state(g, 0)
                neighbours_hi(g, 0, 0)
                neighbours_hi(g, 1, 1)
                first_state(g, 1)
                gate_z(g, 0, 0, reuse=False)
                gate_r(g, 0, 0)
                first_state(g, 2)
                first_state(g, 3)
                for j in (2, 3):
                    slot(g, j, j, first=True)
                    if split_next:
                        split_x(g + 1, 2 * j - 4)
                        split_x(g + 1, 2 * j - 3)
                with act.Fori(1, STEPS) as s:
                    for j in range(GB):
                        slot(g, GB * s + j, j, first=False)

            def turn(g, follow):
                candidate(g, ITEMS - 2, GB - 2)
                if follow:
                    x_unit(g + 1, 0)
                gate_z(g, ITEMS - 1, GB - 1)
                gate_r(g, ITEMS - 1, GB - 1)
                if follow:
                    x_unit(g + 1, 1)
                candidate(g, ITEMS - 1, GB - 1)
                if follow:
                    x_unit(g + 1, 2)
                for j in range(GB):
                    last_norm(g, j)
                    if follow:
                        x_unit(g + 1, 3 + j)
                if follow:
                    x_unit(g + 1, UNITS - 1)
                    conv_rest(g + 1)

            for b in range(GB):
                split_x(0, b)
            act.wait_ge(ld_adj, 16)
            for kt in range(NT):
                sc.copy(adj_hi[:, kt], adj[:, kt]).then_inc(adjhi_ok, 1)
            act.wait_ge(dinv_ok, 1)
            for u in range(UNITS):
                x_unit(0, u)
            act.wait_ge(w_ok, 1)
            conv_rest(0)
            with act.Fori(0, NG - 1) as g:
                gated(g, True)
                turn(g, True)
            gated(NG - 1, False)
            turn(NG - 1, False)

        @block.vector
        def _(dve):
            ve_ = nc.vector
            chained = [0]

            def link(ins):
                chained[0] += 1
                ins.then_inc(w_chain, 1)
                dve.wait_ge(w_chain, chained[0])

            def less_hi(dst, x, hi):
                return ve_.tensor_tensor(dst, x, hi.bitcast(f32), ALU.subtract)

            dve.wait_ge(consts, 6)
            dve.wait_ge(ld_w, 16 * 5)
            ve_.tensor_scalar(cat[:, 0], chw[:, 2], 2.0, None, ALU.mult)
            ve_.tensor_copy(cat[:, 1], chw[:, 1])
            link(ve_.tensor_tensor(cat[:, 2], chw[:, 0], chw[:, 2], ALU.subtract))
            link(ve_.tensor_tensor(cat[:, 2], cat[:, 2], ident[:], ALU.add))
            link(ve_.tensor_copy(cat_hi[:], cat[:]))
            less_hi(cat_lo[:], cat[:], cat_hi[:]).then_inc(cat_ok, 1)
            for b in range(GB):
                dve.wait_ge(xhi_ok, b + 1)
                less_hi(xf_lo[:, b], xf[:, b], xf_hi[:, b]).then_inc(xlo_ok, 1)
            for kt in range(NT):
                dve.wait_ge(adjhi_ok, kt + 1)
                less_hi(adj_lo[:, kt], adj[:, kt], adj_hi[:, kt]).then_inc(adj_split, 1)
            dve.wait_ge(dia_ok, NT)
            link(ve_.tensor_copy(dia_hi[:], dia[:]))
            less_hi(dia_lo[:], dia[:], dia_hi[:]).then_inc(adj_split, 1)
            ve_.tensor_copy(ones_r[:], ones[:]).then_inc(adj_split, 1)
            link(ve_.tensor_tensor(gt[:, GZ:GV + 1], gw[:, :, 0], gw[:, :, 1], ALU.add))
            link(ve_.tensor_tensor(gt[:, GR], gt[:, GR], gt[:, GZ], ALU.subtract))
            link(ve_.tensor_copy(gt[:, U3:U5 + 1], gu[:]))
            link(ve_.tensor_copy(gt_hi[:], gt[:]))
            less_hi(gt_lo[:], gt[:], gt_hi[:])
            ve_.tensor_tensor(bias[:, 0:1], gb[:, 0:1], gb[:, 3:4], ALU.add)
            ve_.tensor_tensor(bias[:, 1:2], gb[:, 1:2], gb[:, 3:4], ALU.add)
            ve_.tensor_tensor(bias[:, 2:3], gb[:, 2:3], gb[:, 4:5], ALU.add).then_inc(w_ok, 1)
            dve.wait_ge(deg_ok, 1)
            link(ve_.tensor_copy(deg[:], ps[:, 0, 0:2 * NT].rearrange("p (t two) -> p t two", two=2)[:, :, 0]))
            link(ve_.tensor_scalar(pos[:], deg[:], 0.0, None, ALU.is_gt))
            link(ve_.tensor_scalar(neg[:], pos[:], -1.0, 1.0, ALU.mult, ALU.add))
            link(ve_.tensor_tensor(safe[:], deg[:], pos[:], ALU.mult))
            ve_.tensor_tensor(safe[:], safe[:], neg[:], ALU.add).then_inc(safe_ok, 1)
            dve.wait_ge(root_ok, 1)
            link(ve_.tensor_tensor(dinv[:], root[:], pos[:], ALU.mult))
            link(ve_.tensor_scalar(ndinv[:], dinv[:], -1.0, None, ALU.mult))
            ve_.tensor_tensor(ndinv2[:], ndinv[:], dinv[:], ALU.mult).then_inc(dinv_ok, 1)
            dve.wait_ge(dinv_ok, 1)

            def neighbours_lo(g, n, j):
                dve.wait_ge(mhi_ok, ITEMS * g + n + 1)
                less_hi(m_lo[:, j % 2], ps[:, M_BANK + j % 2], m_hi[:, j % 2]).then_inc(mlo_ok, 1)

            def update(g, n, j):
                dve.wait_ge(v_ok, ITEMS * g + n + 1)
                ve_.tensor_tensor(vs[:, j % 2], vs[:, j % 2], hT[:, j], ALU.subtract).then_inc(dif_ok, 1)
                dve.wait_ge(dif_ok, ITEMS * g + n + 1)
                ve_.tensor_tensor(vs[:, j % 2], vs[:, j % 2], zs[:, j % 2], ALU.mult).then_inc(upd_ok, 1)
                dve.wait_ge(upd_ok, ITEMS * g + n + 1)
                ve_.tensor_tensor(hT[:, j], hT[:, j], vs[:, j % 2], ALU.add).then_inc(h_ok, 1)

            def reset(g, n, j):
                dve.wait_ge(r_ok, ITEMS * g + n + 1)
                ve_.tensor_tensor(rs[:, j % 2], rs[:, j % 2], hT[:, j], ALU.mult).then_inc(rh_ok, 1)
                dve.wait_ge(rh_ok, ITEMS * g + n + 1)
                ve_.tensor_copy(rh_hi[:, j % 2], rs[:, j % 2]).then_inc(rhhi_ok, 1)
                dve.wait_ge(rhhi_ok, ITEMS * g + n + 1)
                less_hi(rh_lo[:, j % 2], rs[:, j % 2], rh_hi[:, j % 2]).then_inc(rhlo_ok, 1)

            def slot(g, n, j, first, sums=True):
                a, b = (j - 1) % GB, (j - 2) % GB
                if sums:
                    neighbours_lo(g, n - 1, a)
                if not first:
                    dve.wait_ge(hnhi_ok, ITEMS * g + n + 1)
                    less_hi(hn_lo[:, j], t_bank(j), hn_hi[:, j]).then_inc(hnlo_ok, 1)
                update(g, n - 2, b)
                reset(g, n - 1, a)

            def x_unit(g, u):
                nt, bs, banks = unit(u)
                dve.wait_ge(xw1_ok, UNITS * g + u + 1)
                ve_.scalar_tensor_tensor(y2_lo[:, nt, bs], banks[:, :, 0:P], dinv[:, nt:nt + 1],
                                         y2_hi[:, nt, bs].bitcast(f32), ALU.mult, ALU.subtract)
                ve_.tensor_tensor(xw0[:, nt, bs], banks[:, :, 2 * P:3 * P],
                                  chb[:].unsqueeze(1).broadcast_to([P, 2, P]), ALU.add).then_inc(xw0_ok, 1)

            def conv_rest(g):
                def y1_lo_part(nt):
                    dve.wait_ge(y1hi_ok, NT * g + nt + 1)
                    less_hi(y1_lo[:, nt], xw1[:, nt], y1_hi[:, nt]).then_inc(y1lo_ok, 1)

                def node_lo(nt):
                    dve.wait_ge(hnhi_ok, ITEMS * g + nt + 1)
                    less_hi(hn_lo[:, :, nt], hx[:, nt], hn_hi[:, :, nt]).then_inc(hnlo_ok, 1)

                for nt in range(NT):
                    dve.wait_ge(l1_done, NT * g + nt + 1)
                    ve_.scalar_tensor_tensor(xw1[:, nt], ps[:, L1_BANK + nt].rearrange("p (b d) -> p b d", d=P),
                                             ndinv2[:, nt:nt + 1], xw1[:, nt], ALU.mult, ALU.add).then_inc(y1_ok, 1)
                    if nt >= 1:
                        y1_lo_part(nt - 1)
                y1_lo_part(NT - 1)
                for nt in range(NT):
                    dve.wait_ge(l2_done, NT * g + nt + 1)
                    ve_.scalar_tensor_tensor(hx[:, nt], ps[:, L2_BANK + nt].rearrange("p (b d) -> p b d", d=P),
                                             ndinv[:, nt:nt + 1], xw0[:, nt], ALU.mult, ALU.add).then_inc(x1_ok, 1)
                    dve.wait_ge(x1_ok, NT * g + nt + 1)
                    for b in range(GB):
                        ve_.bn_stats(st[:, nt, b, :], hx[:, nt, b, :])
                    dve.drain()
                    for b in range(GB):
                        last = ve_.bn_aggr(mv[:, nt, b, :], st[:, nt, b, :])
                    last.then_inc(mv_ok, 1)
                    if nt >= 2:
                        node_lo(nt - 2)
                node_lo(NT - 2)
                node_lo(NT - 1)

            def gated(g):
                neighbours_lo(g, 0, 0)
                neighbours_lo(g, 1, 1)
                reset(g, 0, 0)
                slot(g, 2, 2, first=True, sums=False)
                slot(g, 3, 3, first=True)
                with dve.Fori(1, STEPS) as s:
                    for j in range(GB):
                        slot(g, GB * s + j, j, first=False)

            def last_sum(g, j, follow):
                dve.wait_ge(t_done, ITEMS * g + ITEMS - GB + j + 1)
                if j >= 2:
                    dve.wait_ge(st_out[j % 2], 16 * (GB // 2 * g + j // 2))
                elif not follow:
                    dve.wait_ge(st_out[j % 2], 16 * (GB // 2 * g))
                ve_.tensor_tensor(yo[:, j % 2], t_bank(j), hx[:, :, j, :], ALU.add).then_inc(yo_ok, 1)
                dve.wait_ge(yo_ok, GB * g + j + 1)
                for t in range(NT):
                    ve_.bn_stats(so[:, j % 2, t, :], yo[:, j % 2, t, :])
                dve.drain()
                for t in range(NT):
                    last = ve_.bn_aggr(mo[:, j % 2, t, :], so[:, j % 2, t, :])
                last.then_inc(mo_ok, 1)

            def turn(g, follow):
                neighbours_lo(g, ITEMS - 1, GB - 1)
                update(g, ITEMS - 2, GB - 2)
                if follow:
                    x_unit(g + 1, 0)
                reset(g, ITEMS - 1, GB - 1)
                if follow:
                    x_unit(g + 1, 1)
                last_sum(g, 0, follow)
                update(g, ITEMS - 1, GB - 1)
                if follow:
                    x_unit(g + 1, 2)
                for j in range(1, GB):
                    last_sum(g, j, follow)
                    if follow:
                        x_unit(g + 1, 2 + j)
                if follow:
                    x_unit(g + 1, UNITS - 2)
                    x_unit(g + 1, UNITS - 1)
                    conv_rest(g + 1)

            for u in range(UNITS):
                x_unit(0, u)
            conv_rest(0)
            with dve.Fori(0, NG - 1) as g:
                gated(g)
                turn(g, True)
            gated(NG - 1)
            turn(NG - 1, False)

        @block.tensor
        def _(pe):
            mm = nc.tensor.matmul

            def x_unit(g, u, free=None):
                nt, bs, banks = unit(u)
                if u == 0:
                    pe.wait_ge(xlo_ok, GB * g + GB)
                if free is not None:
                    pe.wait_ge(*free)
                elif u >= len(X_BANKS):
                    pe.wait_ge(xw0_ok, UNITS * g + u - len(X_BANKS) + 1)
                w_hi, w_lo = (w[:].rearrange("p k d -> p (k d)") for w in (cat_hi, cat_lo))
                rows = slice(nt * P, (nt + 1) * P)
                for i in range(2):
                    bank, b = banks[:, i, 0:NCHEB * P], bs.start + i
                    mm(bank, xf_hi[:, b, rows], w_hi, start=True, stop=False)
                    mm(bank, xf_hi[:, b, rows], w_lo, start=False, stop=False)
                    last = mm(bank, xf_lo[:, b, rows], w_hi, start=False, stop=True)
                last.then_inc(xw_done, 1)

            def aggregate(bank, nt, hi, lo, ready):
                flat = "p b d -> p (b d)"
                for kt in range(NT):
                    ready(kt)
                    a_hi, a_lo = lap(kt, nt)
                    mm(bank, a_hi, hi[:, kt].rearrange(flat), start=kt == 0, stop=False)
                    mm(bank, a_lo, hi[:, kt].rearrange(flat), start=False, stop=False)
                    last = mm(bank, a_hi, lo[:, kt].rearrange(flat), start=False, stop=kt == NT - 1)
                return last

            def conv_rest(g):
                def y2_ready(kt):
                    if kt == 0:
                        pe.wait_ge(xw0_ok, UNITS * g + UNITS - 2)
                    if kt == NT - 1:
                        pe.wait_ge(xw0_ok, UNITS * g + UNITS)

                def y1_ready(kt):
                    pe.wait_ge(y1lo_ok, NT * g + kt + 1)

                def no_wait(kt):
                    pass

                for nt in range(NT):
                    aggregate(ps[:, L1_BANK + nt], nt, y2_hi, y2_lo, no_wait if nt else y2_ready).then_inc(l1_done, 1)
                for nt in range(NT):
                    aggregate(ps[:, L2_BANK + nt], nt, y1_hi, y1_lo, no_wait if nt else y1_ready).then_inc(l2_done, 1)

            def weight(w, bank, hi, lo, start, stop):
                mm(bank, gt_hi[:, w], hi, start=start, stop=False)
                mm(bank, gt_lo[:, w], hi, start=False, stop=False)
                return mm(bank, gt_hi[:, w], lo, start=False, stop=stop)

            def neighbours(g, n, j, part):
                bank = ps[:, M_BANK + j % 2]
                runs = [(hn_hi, kt, a) for kt in range(NT) for a in (adj_hi, adj_lo)]
                runs += [(hn_lo, kt, adj_hi) for kt in range(NT)]
                half = len(runs) // 2
                for i in range(part * half, (part + 1) * half):
                    h, kt, a = runs[i]
                    if i == 0:
                        pe.wait_ge(hnhi_ok, ITEMS * g + n + 1)
                    if i == 2 * NT:
                        pe.wait_ge(hnlo_ok, ITEMS * g + n + 1)
                    last = mm(bank, h[:, j, kt, :], a[:, kt], start=i == 0, stop=i == len(runs) - 1)
                if part == 1:
                    last.then_inc(m_done, 1)

            def first_neighbours(j, kt):
                bank = ps[:, M_BANK + j]
                mm(bank, hn_hi[:, j, kt, :], adj_hi[:, kt], start=kt == 0, stop=False)
                mm(bank, hn_hi[:, j, kt, :], adj_lo[:, kt], start=False, stop=False)
                return mm(bank, hn_lo[:, j, kt, :], adj_hi[:, kt], start=False, stop=kt == NT - 1)

            def gates_z(g, n, j):
                a = j % 2
                pe.wait_ge(hTlo_ok, SPLITS * g + n + 1)
                weight(U3, ps[:, Z_BANK + a], hT_hi[:, j], hT_lo[:, j], True, False)
                pe.wait_ge(mlo_ok, ITEMS * g + n + 1)
                weight(GZ, ps[:, Z_BANK + a], m_hi[:, a], m_lo[:, a], False, True).then_inc(z_done, 1)

            def gates_r(g, n, j):
                a = j % 2
                bank = ps[:, Z_BANK + a]
                pe.wait_ge(z_ok, ITEMS * g + n + 1)
                for i, (w, m) in enumerate(((gt_hi, m_hi), (gt_lo, m_hi), (gt_hi, m_lo))):
                    last = mm(bank, w[:, GR], m[:, a], start=False, stop=i == 2, skip_group_check=True)
                last.then_inc(r_done, 1)

            def cand_m(g, n, j, reuse=True):
                a = j % 2
                if reuse:
                    pe.wait_ge(v_ok, ITEMS * g + n - 1)
                weight(GV, ps[:, V_BANK + a], m_hi[:, a], m_lo[:, a], True, False)

            def cand_h(g, n, j):
                a = j % 2
                bank = ps[:, V_BANK + a]
                pe.wait_ge(rhhi_ok, ITEMS * g + n + 1)
                mm(bank, gt_hi[:, U5], rh_hi[:, a], start=False, stop=False)
                mm(bank, gt_lo[:, U5], rh_hi[:, a], start=False, stop=False)
                pe.wait_ge(rhlo_ok, ITEMS * g + n + 1)
                mm(bank, gt_hi[:, U5], rh_lo[:, a], start=False, stop=True).then_inc(v_done, 1)

            def to_node(g, n, j):
                pe.wait_ge(h_ok, ITEMS * g + n + 1)
                for t in range(NT):
                    last = nc.tensor.transpose(ps[:, T_BANK + j % 2, t * P:(t + 1) * P],
                                               hT[:, j, t * P:(t + 1) * P], ident[:])
                last.then_inc(t_done, 1)

            def slot(g, n, j, first):
                a, b = (j - 1) % GB, (j - 2) % GB
                if not first:
                    pe.wait_ge(hnlo_ok, ITEMS * g + n - 1)
                    to_node(g, n - GB, j)
                cand_h(g, n - 2, b)
                gates_z(g, n - 1, a)
                neighbours(g, n, j, 0)
                gates_r(g, n - 1, a)
                cand_m(g, n - 1, a, reuse=not (first and j <= 2))
                neighbours(g, n, j, 1)

            def gated(g):
                for kt in range(NT - 1):
                    pe.wait_ge(hnlo_ok, ITEMS * g + kt + 1)
                    for j in range(2):
                        first_neighbours(j, kt)
                pe.wait_ge(x1_ok, NT * g + NT)
                for t in range(NT):
                    if t == NT - 1:
                        pe.wait_ge(hx_ok, NT * g + NT)
                    for j in range(GB):
                        last = nc.tensor.transpose(ps[:, j, t * P:(t + 1) * P], hx[:, t, j, :], ident[:])
                        if t == NT - 1:
                            last.then_inc(hxT_done, 1)
                pe.wait_ge(hnlo_ok, ITEMS * g + NT)
                for j in range(2):
                    first_neighbours(j, NT - 1).then_inc(m_done, 1)
                gates_z(g, 0, 0)
                gates_r(g, 0, 0)
                pe.wait_ge(hThi_ok, SPLITS * g + GB)
                cand_m(g, 0, 0, reuse=False)
                slot(g, 2, 2, first=True)
                slot(g, 3, 3, first=True)
                with pe.Fori(1, STEPS) as s:
                    for j in range(GB):
                        slot(g, GB * s + j, j, first=False)

            def turn(g, follow):
                ends = ITEMS * g + ITEMS
                cand_h(g, ITEMS - 2, GB - 2)
                pe.wait_ge(hnlo_ok, ends)
                to_node(g, ITEMS - 4, 0)
                if follow:
                    x_unit(g + 1, 0, free=(mlo_ok, ends))
                gates_z(g, ITEMS - 1, GB - 1)
                to_node(g, ITEMS - 3, 1)
                gates_r(g, ITEMS - 1, GB - 1)
                cand_m(g, ITEMS - 1, GB - 1)
                if follow:
                    x_unit(g + 1, 1, free=(r_ok, ends))
                cand_h(g, ITEMS - 1, GB - 1)
                pe.wait_ge(yo_ok, GB * g + 1)
                to_node(g, ITEMS - 2, 2)
                if follow:
                    x_unit(g + 1, 2, free=(v_ok, ends))
                    x_unit(g + 1, 3)
                pe.wait_ge(yo_ok, GB * g + 2)
                to_node(g, ITEMS - 1, 3)
                if follow:
                    for u in range(4, UNITS):
                        x_unit(g + 1, u)
                    conv_rest(g + 1)

            pe.wait_ge(cat_ok, 1)
            for u in range(3):
                x_unit(0, u)
            pe.wait_ge(adj_split, NT + 2)
            for nt in range(NT):
                for kt in range(NT):
                    hi, lo = lap(kt, nt)
                    mm(ps[:, 0, 2 * nt:2 * nt + 2], hi, ones_r[:], start=kt == 0, stop=False)
                    last = mm(ps[:, 0, 2 * nt:2 * nt + 2], lo, ones_r[:], start=False, stop=kt == NT - 1)
            last.then_inc(deg_ok, 1)
            for u in range(3, UNITS):
                x_unit(0, u)
            conv_rest(0)
            with pe.Fori(0, NG - 1) as g:
                gated(g)
                turn(g, True)
            gated(NG - 1)
            turn(NG - 1, False)


def kernel(**inputs):
    import numpy as np
    import concourse.bacc as bacc
    from concourse.bass_utils import run_bass_kernel_spmd

    def arr(name):
        return np.asarray(inputs[name])

    P = 128
    x = arr("x")
    xT = np.ascontiguousarray(x.transpose(0, 2, 1))
    adjT = np.ascontiguousarray(arr("adj").T)
    cheb_w = np.ascontiguousarray(arr("L0_gnn_Ws").transpose(1, 0, 2))
    gate_w = np.ascontiguousarray(np.stack([arr(f"L1_gnn_w{k}_w").T.reshape(2, P, P) for k in (3, 4, 5)])
                                  .transpose(2, 0, 1, 3))
    gate_u = np.ascontiguousarray(np.stack([arr(f"L1_gnn_u{k}_w").T for k in (3, 5)]).transpose(1, 0, 2))
    gate_b = np.ascontiguousarray(np.stack([arr(f"L1_gnn_{k}_b") for k in ("w3", "w4", "w5", "u3", "u5")]).T)
    cheb_b = arr("L0_gnn_bias")
    arrays = {"xT": xT, "adjT": adjT, "cheb_w": cheb_w, "gate_w": gate_w, "gate_u": gate_u,
              "gate_b": gate_b, "cheb_b": cheb_b}

    nc = bacc.Bacc("TRN2", target_bir_lowering=False, num_devices=1)
    args = [nc.dram_tensor(f"in_{n}", a.shape, mybir.dt.from_np(a.dtype), kind="ExternalInput").ap()
            for n, a in arrays.items()]
    out = nc.dram_tensor("out_0", x.shape, mybir.dt.float32, kind="ExternalOutput").ap()
    cheb_gated_graph_kernel(nc, *args, out)
    r = run_bass_kernel_spmd(nc, [{f"in_{n}": a for n, a in arrays.items()}], core_ids=[0])
    return r.results[0]["out_0"]
```

```python
import concourse.bass as bass
from concourse import mybir
from contextlib import ExitStack


def cheb_gated_graph_kernel(nc, xT, adjT, cheb_w, gate_w, gate_u, gate_b, cheb_b, out):
    f32, f32r = mybir.dt.float32, mybir.dt.float32r
    ALU = mybir.AluOpType
    ACT = mybir.ActivationFunctionType

    P = 128
    B, F, N = xT.shape
    NT = N // P
    GB = 4
    NG = B // GB
    STEPS = 5
    ITEMS = STEPS * GB
    EPS = 1e-5
    NCHEB = 3
    SPLITS = ITEMS + 2

    ctx = ExitStack()
    with ctx:
        def sb(name, shape, dt=f32):
            return ctx.enter_context(nc.sbuf_tensor(name, shape, dt))

        def sem(name):
            return ctx.enter_context(nc.semaphore(name))

        yx = sb("yx", [P, 2, NT, GB, P])
        adj = yx[:, 0].rearrange("p t b d -> p t (b d)")
        adj_hi = sb("adj_hi", [P, NT, N], f32r)
        adj_lo = sb("adj_lo", [P, NT, N], f32r)
        dia_hi = sb("dia_hi", [P, NT, P], f32r)
        dia_lo = sb("dia_lo", [P, NT, P], f32r)
        ident = sb("ident", [P, P])
        ones = sb("ones", [P, 2])
        warm = sb("warm", [P, 1])
        ones_r = sb("ones_r", [P, 2], f32r)
        chw = sb("chw", [P, NCHEB, P])
        cat = sb("cat", [P, NCHEB, P])
        cat_hi = sb("cat_hi", [P, NCHEB, P], f32r)
        cat_lo = sb("cat_lo", [P, NCHEB, P], f32r)
        gw = sb("gw", [P, 3, 2, P])
        gu = sb("gu", [P, 2, P])
        GZ, GR, GV, U3, U5 = range(5)
        gt = sb("gt", [P, 5, P])
        gt_hi = sb("gt_hi", [P, 5, P], f32r)
        gt_lo = sb("gt_lo", [P, 5, P], f32r)
        gb = sb("gb", [P, 5])
        bias = sb("bias", [P, 3])
        chb = sb("chb", [P, P])
        deg_row = sb("deg_row", [2, N])
        pos = sb("pos", [P, NT])
        neg = sb("neg", [P, NT])
        safe = sb("safe", [P, NT])
        zero = sb("zero", [P, GB])
        root = sb("root", [P, NT])
        mhalf = sb("mhalf", [P, GB])
        eps = sb("eps", [P, GB])
        dinv = sb("dinv", [P, NT])
        ndinv = sb("ndinv", [P, NT])
        ndinv2 = sb("ndinv2", [P, NT])

        xf = sb("xf", [P, GB, N])
        xf_hi = sb("xf_hi", [P, GB, N], f32r)
        xf_lo = sb("xf_lo", [P, GB, N], f32r)
        y2_hi = sb("y2_hi", [P, NT, GB, P], f32r)
        y2_lo = sb("y2_lo", [P, NT, GB, P], f32r)
        xw1 = yx[:, 1]
        xw0 = sb("xw0", [P, NT, GB, P])
        y1_hi = sb("y1_hi", [P, NT, GB, P], f32r)
        y1_lo = sb("y1_lo", [P, NT, GB, P], f32r)
        hx = sb("hx", [P, NT, GB, P])
        st = sb("st", [P, NT, GB, 6])
        mv = sb("mv", [P, NT, GB, 2])
        ve = sb("ve", [P, NT, GB])
        rstd = sb("rstd", [P, NT, GB])
        mr = sb("mr", [P, NT, GB])
        nmr = sb("nmr", [P, NT, GB])

        hT = sb("hT", [P, GB, N])
        hT_hi = sb("hT_hi", [P, GB, N], f32r)
        hT_lo = sb("hT_lo", [P, GB, N], f32r)
        hn_hi = sb("hn_hi", [P, GB, NT, P], f32r)
        hn_lo = sb("hn_lo", [P, GB, NT, P], f32r)
        m_hi = sb("m_hi", [P, 2, N], f32r)
        m_lo = sb("m_lo", [P, 2, N], f32r)
        zs = sb("zs", [P, 2, N])
        rs = sb("rs", [P, 2, N])
        vs = sb("vs", [P, 2, N])
        rh_hi = sb("rh_hi", [P, 2, N], f32r)
        rh_lo = sb("rh_lo", [P, 2, N], f32r)
        yo = sb("yo", [P, NT, P])
        so = sb("so", [P, GB, NT, 6])
        mo = sb("mo", [P, GB, NT, 2])
        vo = sb("vo", [P, GB, NT])
        ro = sb("ro", [P, GB, NT])
        mro = sb("mro", [P, GB, NT])
        nmro = sb("nmro", [P, GB, NT])

        ps = ctx.enter_context(nc.psum_tensor("ps", [P, 8, N], f32))
        T_BANK, V_BANK, Z_BANK, M_BANK = 0, 2, 4, 6
        UNITS = NT * GB // 2
        X_BANKS = (M_BANK, Z_BANK, M_BANK, Z_BANK, V_BANK, M_BANK, Z_BANK, M_BANK)
        X_BEFORE = {u: max(v for v in range(u) if X_BANKS[v] == X_BANKS[u])
                    for u in range(UNITS) if X_BANKS[u] in X_BANKS[:u]}
        L1_BANKS = (V_BANK, V_BANK + 1, Z_BANK, Z_BANK + 1)
        HX_BANKS = (T_BANK, Z_BANK + 1, V_BANK, T_BANK + 1)
        PARTS = [(nt, slice(0, GB), bank) for nt, bank in zip(range(NT - 1), (M_BANK, M_BANK + 1, Z_BANK))]
        PARTS += [(NT - 1, slice(0, 2), V_BANK + 1), (NT - 1, slice(2, GB), Z_BANK)]
        NP = len(PARTS)

        ld_adj = [sem(f"ld_adj{kt}") for kt in range(NT)]
        ld_cat, ld_w, ld_x = sem("ld_cat"), sem("ld_w"), sem("ld_x")
        ld_x01 = sem("ld_x01")
        st_out = sem("st_out")
        st_last = sem("st_last")
        consts = sem("consts")
        dia_ok = sem("dia_ok")
        adjhi_ok = sem("adjhi_ok")
        ones_ok = sem("ones_ok")
        adj_split = sem("adj_split")
        w_chain = sem("w_chain")
        cat_ok = sem("cat_ok")
        w_ok = sem("w_ok")
        row_done = sem("row_done")
        row_ok = sem("row_ok")
        deg_ok = sem("deg_ok")
        safe_ok = sem("safe_ok")
        root_ok = sem("root_ok")
        dinv_ok = sem("dinv_ok")
        xhi_ok = sem("xhi_ok")
        xlo_ok = sem("xlo_ok")
        xw_done = sem("xw_done")
        y2_ok = sem("y2_ok")
        xw_ok = sem("xw_ok")
        y2hi_ok = sem("y2hi_ok")
        y2lo_ok = sem("y2lo_ok")
        base_ok = sem("base_ok")
        l1_done = sem("l1_done")
        y1_ok = sem("y1_ok")
        y1hi_ok = sem("y1hi_ok")
        y1lo_ok = sem("y1lo_ok")
        y1lo_last = sem("y1lo_last")
        l2_done = sem("l2_done")
        x1_ok = sem("x1_ok")
        mv_ok = sem("mv_ok")
        ve_ok = sem("ve_ok")
        rstd_ok = sem("rstd_ok")
        mr_ok = sem("mr_ok")
        nmr_ok = sem("nmr_ok")
        hx_ok = sem("hx_ok")
        hxl_ok = sem("hxl_ok")
        half_hi, half_ok = sem("half_hi"), sem("half_ok")
        hxT_done = sem("hxT_done")
        hnhi_ok, hnlo_ok = sem("hnhi_ok"), sem("hnlo_ok")
        hThi_ok, hTlo_ok = sem("hThi_ok"), sem("hTlo_ok")
        m_done, z_done, r_done, v_done = sem("m_done"), sem("z_done"), sem("r_done"), sem("v_done")
        t_done = sem("t_done")
        mhi_ok, mlo_ok = sem("mhi_ok"), sem("mlo_ok")
        z_ok, r_ok, v_ok = sem("z_ok"), sem("r_ok"), sem("v_ok")
        rh_ok, rhhi_ok, rhlo_ok = sem("rh_ok"), sem("rhhi_ok"), sem("rhlo_ok")
        dif_ok, upd_ok, h_ok = sem("dif_ok"), sem("upd_ok"), sem("h_ok")
        sum_ok, mo_ok = sem("sum_ok"), sem("mo_ok")
        vo_ok, ro_ok, mro_ok, nmro_ok = sem("vo_ok"), sem("ro_ok"), sem("mro_ok"), sem("nmro_ok")
        out_ok = sem("out_ok")
        end_ok = sem("end_ok")

        block = ctx.enter_context(nc.Block())

        def lap(kt, nt):
            if kt == nt:
                return dia_hi[:, kt, :], dia_lo[:, kt, :]
            cols = slice(nt * P, (nt + 1) * P)
            return adj_hi[:, kt, cols], adj_lo[:, kt, cols]

        def unit(u):
            nt, b = u // 2, 2 * (u % 2)
            bank = X_BANKS[u]
            return nt, slice(b, b + 2), ps[:, bank:bank + 2]

        def t_bank(j):
            return ps[:, T_BANK + j % 2].rearrange("p (t d) -> p t d", d=P)

        @block.sync
        def _(sp):
            def load_x(g):
                sp.dma_start(xf[:], xT[GB * g:GB * g + GB].rearrange("b f n -> f b n")).then_inc(ld_x, 16)

            for kt in range(NT):
                sp.dma_start(adj[:, kt], adjT[kt * P:(kt + 1) * P]).then_inc(ld_adj[kt], 16)
            sp.dma_start(chw[:], cheb_w).then_inc(ld_cat, 16)
            sp.dma_start(xf[:, 0:2], xT[0:2].rearrange("b f n -> f b n")).then_inc(ld_x01, 16)
            sp.dma_start(xf[:, 2:GB], xT[2:GB].rearrange("b f n -> f b n")).then_inc(ld_x, 16)
            sp.dma_start(gw[:], gate_w).then_inc(ld_w, 16)
            sp.dma_start(gu[:], gate_u).then_inc(ld_w, 16)
            sp.dma_start(gb[:], gate_b).then_inc(ld_w, 16)
            sp.dma_start(chb[:], cheb_b.partition_broadcast(P)).then_inc(ld_w, 16)
            for g in range(NG):
                if g + 1 < NG:
                    sp.wait_ge(xhi_ok, GB * g + GB)
                    sp.wait_ge(xlo_ok, GB * g + GB)
                    load_x(g + 1)
                for j in range(GB):
                    if j == GB - 1 and g == NG - 1:
                        sp.wait_ge(end_ok, 1)
                    else:
                        sp.wait_ge(out_ok, GB * g + j + 1)
                    src, stored = (hx[:, :, j, :], st_out) if j < GB - 1 else (yo[:], st_last)
                    sp.dma_start(out[GB * g + j].rearrange("(t p) d -> p t d", p=P), src).then_inc(stored, 16)
            sp.wait_ge(st_out, 16 * (GB - 1) * NG)
            sp.wait_ge(st_last, 16 * NG)

        @block.gpsimd
        def _(pool):
            gp = nc.gpsimd
            gp.memset(ones[:], 1.0).then_inc(consts, 1)
            gp.memset(mhalf[:], -0.5).then_inc(consts, 1)
            gp.memset(eps[:], EPS).then_inc(consts, 1)
            gp.memset(zero[:], 0.0).then_inc(consts, 1)
            gp.memset(ident[:], 0.0).then_inc(consts, 1)
            pool.wait_ge(consts, 5)
            gp.affine_select(out=ident[:], in_=ident[:], compare_op=ALU.not_equal, fill=1.0, base=0,
                             pattern=[[-1, P]], channel_multiplier=1).then_inc(consts, 1)
            for kt in range(NT):
                cols = slice(kt * P, (kt + 1) * P)
                for src, dst, ready in ((adj_hi, dia_hi, adjhi_ok), (adj_lo, dia_lo, adj_split)):
                    pool.wait_ge(ready, kt + 1)
                    gp.affine_select(out=dst[:, kt, :], in_=src[:, kt, cols],
                                     compare_op=ALU.not_equal, fill=0.0, base=0,
                                     pattern=[[-1, P]], channel_multiplier=1).then_inc(dia_ok, 1)
            pool.wait_ge(xhi_ok, 1)
            gp.tensor_tensor(xf_lo[:, 0], xf[:, 0], xf_hi[:, 0].bitcast(f32), ALU.subtract).then_inc(xlo_ok, 1)
            pool.wait_ge(safe_ok, 1)
            gp.tensor_tensor(root[:], safe[:], mhalf[:, 0:NT], ALU.pow).then_inc(root_ok, 1)

            def scale_shift(count, var, mean, v, r, m, nm, ready, sems, shift):
                v_sem, r_sem, m_sem, nm_sem = sems
                pool.wait_ge(ready, count)
                gp.tensor_tensor(v, var, eps[:, 0:var.shape[1]], ALU.add).then_inc(v_sem, 1)
                pool.wait_ge(v_sem, count)
                gp.tensor_tensor(r, v, mhalf[:, 0:var.shape[1]], ALU.pow).then_inc(r_sem, 1)
                if shift is None:
                    return
                pool.wait_ge(r_sem, count)
                gp.tensor_tensor(m, mean, r, ALU.mult).then_inc(m_sem, 1)
                pool.wait_ge(m_sem, shift)
                gp.tensor_tensor(nm, zero[:], m, ALU.subtract).then_inc(nm_sem, 1)

            def base(g, nt):
                pool.wait_ge(xw_ok, UNITS * g + 2 * nt + 2)
                gp.tensor_tensor(xw0[:, nt], xw0[:, nt], chb[:].unsqueeze(1).broadcast_to([P, GB, P]),
                                 ALU.add).then_inc(base_ok, 1)

            def first_norm(g):
                for i, (nt, bs, _) in enumerate(PARTS):
                    if i == 1:
                        base(g, NT - 1)
                    scale_shift(NP * g + i + 1, mv[:, nt, bs, 1], mv[:, nt, bs, 0], ve[:, nt, bs],
                                rstd[:, nt, bs], mr[:, nt, bs], nmr[:, nt, bs], mv_ok,
                                (ve_ok, rstd_ok, mr_ok, nmr_ok),
                                (NT - 1) * g + nt + 1 if nt < NT - 1 else None)

            def y2_lo_part(g, u):
                nt, bs, _ = unit(u)
                pool.wait_ge(y2hi_ok, UNITS * g + u + 1)
                gp.tensor_tensor(y2_lo[:, nt, bs], yx[:, 0, nt, bs], y2_hi[:, nt, bs].bitcast(f32),
                                 ALU.subtract).then_inc(y2lo_ok, 1)

            def y1_lo_part(g, nt):
                pool.wait_ge(y1hi_ok, NT * g + nt + 1)
                gp.tensor_tensor(y1_lo[:, nt], xw1[:, nt], y1_hi[:, nt].bitcast(f32),
                                 ALU.subtract).then_inc(y1lo_ok, 1)

            def last_norm(g, j):
                scale_shift(GB * g + j + 1, mo[:, j, :, 1], mo[:, j, :, 0], vo[:, j], ro[:, j],
                            mro[:, j], nmro[:, j], mo_ok, (vo_ok, ro_ok, mro_ok, nmro_ok), GB * g + j + 1)

            def state_lo(split, j):
                pool.wait_ge(hThi_ok, split + 1)
                gp.tensor_tensor(hT_lo[:, j], hT[:, j], hT_hi[:, j].bitcast(f32), ALU.subtract).then_inc(hTlo_ok, 1)

            def gated(g, split_next):
                pool.wait_ge(hTlo_ok, SPLITS * g + 2)
                for j in range(2, GB):
                    state_lo(SPLITS * g + j, j)
                for j in range(2):
                    state_lo(SPLITS * g + GB + j, j)
                with pool.Fori(1, STEPS - 1) as s:
                    for j in range(GB):
                        state_lo(SPLITS * g + GB * s + j + 2, (j + 2) % GB)
                for j in range(GB):
                    state_lo(SPLITS * g + GB * (STEPS - 1) + j + 2, (j + 2) % GB)
                    if split_next:
                        pool.wait_ge(xhi_ok, GB * g + GB + j + 1)
                        gp.tensor_tensor(xf_lo[:, j], xf[:, j], xf_hi[:, j].bitcast(f32),
                                         ALU.subtract).then_inc(xlo_ok, 1)

            for u in range(UNITS):
                y2_lo_part(0, u)
            pool.wait_ge(ld_w, 16 * 4)
            for nt in range(NT - 1):
                base(0, nt)
                y1_lo_part(0, nt)
            first_norm(0)
            with pool.Fori(0, NG - 1) as g:
                gated(g, True)
                for u in range(UNITS):
                    y2_lo_part(g + 1, u)
                last_norm(g, 0)
                base(g + 1, 0)
                last_norm(g, 1)
                y1_lo_part(g + 1, 0)
                base(g + 1, 1)
                last_norm(g, 2)
                y1_lo_part(g + 1, 1)
                y1_lo_part(g + 1, 2)
                last_norm(g, 3)
                base(g + 1, NT - 2)
                first_norm(g + 1)
            gated(NG - 1, False)
            n, j = ITEMS - 2, GB - 2
            end = ITEMS * (NG - 1) + n
            pool.wait_ge(v_ok, end + 1)
            pool.wait_ge(h_ok, end)
            gp.tensor_tensor(vs[:, j % 2], vs[:, j % 2], hT[:, j], ALU.subtract).then_inc(dif_ok, 1)
            pool.wait_ge(dif_ok, end + 1)
            gp.tensor_tensor(vs[:, j % 2], vs[:, j % 2], zs[:, j % 2], ALU.mult).then_inc(upd_ok, 1)
            pool.wait_ge(upd_ok, end + 1)
            gp.tensor_tensor(hT[:, j], hT[:, j], vs[:, j % 2], ALU.add).then_inc(h_ok, 1)
            for j in range(GB):
                last_norm(NG - 1, j)

        @block.scalar
        def _(act):
            sc = nc.scalar

            def candidate(g, n, j):
                act.wait_ge(v_done, ITEMS * g + n + 1)
                sc.activation(vs[:, j % 2], ps[:, V_BANK + j % 2], ACT.Tanh, bias=bias[:, 2:3]).then_inc(v_ok, 1)

            def gate_z(g, n, j, reuse=True):
                act.wait_ge(z_done, ITEMS * g + n + 1)
                if reuse:
                    act.wait_ge(upd_ok, ITEMS * g + n - 1)
                sc.activation(zs[:, j % 2], ps[:, Z_BANK + j % 2], ACT.Sigmoid, bias=bias[:, 0:1]).then_inc(z_ok, 1)

            def gate_r(g, n, j):
                act.wait_ge(r_done, ITEMS * g + n + 1)
                sc.activation(rs[:, j % 2], ps[:, Z_BANK + j % 2], ACT.Sigmoid, bias=bias[:, 1:2]).then_inc(r_ok, 1)

            def state_hi(g, n, j):
                act.wait_ge(h_ok, ITEMS * g + n + 1)
                sc.copy(hT_hi[:, j], hT[:, j]).then_inc(hThi_ok, 1)

            def neighbours_hi(g, n, j):
                act.wait_ge(m_done, ITEMS * g + n + 1)
                sc.copy(m_hi[:, j % 2], ps[:, M_BANK + j % 2]).then_inc(mhi_ok, 1)

            def slot(g, n, j):
                a, b = (j - 1) % GB, (j - 2) % GB
                act.wait_ge(t_done, ITEMS * g + n - GB + 1)
                sc.copy(hn_hi[:, j], t_bank(j)).then_inc(hnhi_ok, 1)
                candidate(g, n - 2, b)
                gate_z(g, n - 1, a)
                gate_r(g, n - 1, a)
                state_hi(g, n - 2, b)
                neighbours_hi(g, n, j)

            def first_state(g, j):
                act.wait_ge(hxT_done, GB * g + j + 1)
                sc.copy(hT[:, j], ps[:, HX_BANKS[j]])
                sc.copy(hT_hi[:, j], ps[:, HX_BANKS[j]]).then_inc(hThi_ok, 1)

            def split_x(g, b, loaded):
                act.wait_ge(*loaded)
                sc.copy(xf_hi[:, b], xf[:, b]).then_inc(xhi_ok, 1)

            def x_unit(g, u):
                nt, bs, banks = unit(u)
                act.wait_ge(xw_done, UNITS * g + u + 1)
                sc.activation(yx[:, :, nt, bs].rearrange("p k b d -> p b k d"),
                              banks[:, :, 0:2 * P].rearrange("p b (k d) -> p b k d", d=P),
                              ACT.Copy, scale=dinv[:, nt:nt + 1]).then_inc(y2_ok, 1)
                sc.copy(xw0[:, nt, bs], banks[:, :, 2 * P:3 * P]).then_inc(xw_ok, 1)

            def last_norm(g, j):
                act.wait_ge(nmro_ok, GB * g + j + 1)
                for t in range(NT):
                    last = sc.activation(hx[:, t, j] if j < GB - 1 else yo[:, t], hx[:, t, j], ACT.Identity,
                                         scale=ro[:, j, t:t + 1], bias=nmro[:, j, t:t + 1])
                last.then_inc(out_ok, 1)

            def conv_rest(g, between=None):
                for nt in range(NT):
                    act.wait_ge(y1_ok, NT * g + nt + 1)
                    sc.copy(y1_hi[:, nt], xw1[:, nt]).then_inc(y1hi_ok, 1)
                    if between and nt == 0:
                        between(1)
                if between:
                    between(2)
                    between(3)
                    act.wait_ge(out_ok, GB * g)
                    act.wait_ge(st_out, 16 * (GB - 1) * g)
                for nt in range(NT - 1):
                    act.wait_ge(nmr_ok, (NT - 1) * g + nt + 1)
                    for b in range(GB):
                        last = sc.activation(hx[:, nt, b], xw0[:, nt, b], ACT.Identity,
                                             scale=rstd[:, nt, b:b + 1], bias=nmr[:, nt, b:b + 1])
                    last.then_inc(hx_ok, 1)
                    act.wait_ge(hx_ok, (NT - 1) * g + nt + 1)
                    sc.copy(hn_hi[:, :, nt], hx[:, nt]).then_inc(hnhi_ok, 1)
                if between:
                    act.wait_ge(st_last, 16 * g)

            def gated(g, split_next):
                first_state(g, 0)
                first_state(g, 1)
                neighbours_hi(g, 0, 0)
                neighbours_hi(g, 1, 1)
                gate_z(g, 0, 0, reuse=False)
                first_state(g, 2)
                gate_r(g, 0, 0)
                gate_z(g, 1, 1, reuse=False)
                first_state(g, 3)
                gate_r(g, 1, 1)
                candidate(g, 0, 0)
                neighbours_hi(g, 2, 2)
                candidate(g, 1, 1)
                gate_z(g, 2, 2)
                state_hi(g, 0, 0)
                gate_r(g, 2, 2)
                state_hi(g, 1, 1)
                neighbours_hi(g, 3, 3)
                with act.Fori(1, STEPS - 1) as s:
                    for j in range(GB):
                        slot(g, GB * s + j, j)
                for j in range(GB):
                    slot(g, GB * (STEPS - 1) + j, j)
                    if split_next:
                        split_x(g + 1, j, (ld_x, 16 * g + 32))

            def turn(g, follow):
                candidate(g, ITEMS - 2, GB - 2)
                gate_z(g, ITEMS - 1, GB - 1)
                gate_r(g, ITEMS - 1, GB - 1)
                if follow:
                    x_unit(g + 1, 0)
                    x_unit(g + 1, 1)
                candidate(g, ITEMS - 1, GB - 1)
                if follow:
                    for u in range(2, UNITS):
                        x_unit(g + 1, u)
                    last_norm(g, 0)
                    conv_rest(g + 1, lambda j: last_norm(g, j))
                else:
                    for j in range(GB - 1):
                        last_norm(g, j)

            act.wait_ge(consts, 1)
            sc.activation(warm[:], ones[:, 0:1], ACT.Sigmoid)
            for kt in range(NT):
                act.wait_ge(ld_adj[kt], 16)
                sc.copy(adj_hi[:, kt], adj[:, kt]).then_inc(adjhi_ok, 1)
            for b in range(GB):
                split_x(0, b, (ld_x01, 16) if b < 2 else (ld_x, 16))
            act.wait_ge(dinv_ok, 1)
            for u in range(UNITS):
                x_unit(0, u)
            act.wait_ge(w_ok, 1)
            conv_rest(0)
            with act.Fori(0, NG - 1) as g:
                gated(g, True)
                turn(g, True)
            gated(NG - 1, False)
            turn(NG - 1, False)

        @block.vector
        def _(dve):
            ve_ = nc.vector
            chained = [0]

            def link(ins):
                chained[0] += 1
                ins.then_inc(w_chain, 1)
                dve.wait_ge(w_chain, chained[0])

            def less_hi(dst, x, hi):
                return ve_.tensor_tensor(dst, x, hi.bitcast(f32), ALU.subtract)

            dve.wait_ge(consts, 6)
            ve_.tensor_copy(ones_r[:], ones[:]).then_inc(ones_ok, 1)
            for kt in range(NT):
                dve.wait_ge(adjhi_ok, kt + 1)
                less_hi(adj_lo[:, kt], adj[:, kt], adj_hi[:, kt]).then_inc(adj_split, 1)
            dve.wait_ge(ld_cat, 16)
            ve_.tensor_scalar(cat[:, 0], chw[:, 2], 2.0, None, ALU.mult)
            ve_.tensor_copy(cat[:, 1], chw[:, 1])
            link(ve_.tensor_tensor(cat[:, 2], chw[:, 0], chw[:, 2], ALU.subtract))
            link(ve_.tensor_tensor(cat[:, 2], cat[:, 2], ident[:], ALU.add))
            link(ve_.tensor_copy(cat_hi[:], cat[:]))
            less_hi(cat_lo[:], cat[:], cat_hi[:]).then_inc(cat_ok, 1)

            def first_x_lo(b):
                dve.wait_ge(xhi_ok, b + 1)
                dve.wait_ge(xlo_ok, b)
                less_hi(xf_lo[:, b], xf[:, b], xf_hi[:, b]).then_inc(xlo_ok, 1)

            dve.wait_ge(row_done, 1)
            ve_.tensor_copy(deg_row[:].rearrange("p (t n) -> p t n", n=P), ps[0:2, 0:NT, 0:P]).then_inc(row_ok, 1)
            first_x_lo(1)
            dve.wait_ge(deg_ok, 1)
            deg = ps[:, 0, 0:2 * NT].rearrange("p (t two) -> p t two", two=2)[:, :, 0]
            ve_.tensor_scalar(pos[:], deg, 0.0, None, ALU.is_gt)
            link(ve_.tensor_scalar(neg[:], deg, 0.0, None, ALU.is_le))
            ve_.tensor_tensor(safe[:], deg, neg[:], ALU.max).then_inc(safe_ok, 1)
            first_x_lo(2)
            first_x_lo(3)
            dve.wait_ge(root_ok, 1)
            link(ve_.tensor_tensor(dinv[:], root[:], pos[:], ALU.mult))
            ve_.tensor_scalar(ndinv[:], dinv[:], -1.0, None, ALU.mult).then_inc(dinv_ok, 1)
            dve.wait_ge(dinv_ok, 1)
            link(ve_.tensor_tensor(ndinv2[:], ndinv[:], dinv[:], ALU.mult))

            def gate_weights():
                dve.wait_ge(ld_w, 16 * 4)
                link(ve_.tensor_tensor(gt[:, GZ:GV + 1], gw[:, :, 0], gw[:, :, 1], ALU.add))
                link(ve_.tensor_tensor(gt[:, GR], gt[:, GR], gt[:, GZ], ALU.subtract))
                link(ve_.tensor_copy(gt[:, U3:U5 + 1], gu[:]))
                link(ve_.tensor_copy(gt_hi[:], gt[:]))
                less_hi(gt_lo[:], gt[:], gt_hi[:])
                ve_.tensor_tensor(bias[:, 0:1], gb[:, 0:1], gb[:, 3:4], ALU.add)
                ve_.tensor_tensor(bias[:, 1:2], gb[:, 1:2], gb[:, 3:4], ALU.add)
                ve_.tensor_tensor(bias[:, 2:3], gb[:, 2:3], gb[:, 4:5], ALU.add).then_inc(w_ok, 1)

            def neighbours_lo(g, n, j):
                dve.wait_ge(mhi_ok, ITEMS * g + n + 1)
                less_hi(m_lo[:, j % 2], ps[:, M_BANK + j % 2], m_hi[:, j % 2]).then_inc(mlo_ok, 1)

            def difference(g, n, j):
                dve.wait_ge(v_ok, ITEMS * g + n + 1)
                ve_.tensor_tensor(vs[:, j % 2], vs[:, j % 2], hT[:, j], ALU.subtract).then_inc(dif_ok, 1)

            def mix(g, n, j):
                dve.wait_ge(dif_ok, ITEMS * g + n + 1)
                ve_.tensor_tensor(vs[:, j % 2], vs[:, j % 2], zs[:, j % 2], ALU.mult).then_inc(upd_ok, 1)
                dve.wait_ge(upd_ok, ITEMS * g + n + 1)
                ve_.tensor_tensor(hT[:, j], hT[:, j], vs[:, j % 2], ALU.add).then_inc(h_ok, 1)

            def update(g, n, j):
                difference(g, n, j)
                mix(g, n, j)

            def reset(g, n, j):
                dve.wait_ge(r_ok, ITEMS * g + n + 1)
                ve_.tensor_tensor(rs[:, j % 2], rs[:, j % 2], hT[:, j], ALU.mult).then_inc(rh_ok, 1)
                dve.wait_ge(rh_ok, ITEMS * g + n + 1)
                ve_.tensor_copy(rh_hi[:, j % 2], rs[:, j % 2]).then_inc(rhhi_ok, 1)
                dve.wait_ge(rhhi_ok, ITEMS * g + n + 1)
                less_hi(rh_lo[:, j % 2], rs[:, j % 2], rh_hi[:, j % 2]).then_inc(rhlo_ok, 1)

            def slot(g, n, j):
                a, b = (j - 1) % GB, (j - 2) % GB
                neighbours_lo(g, n - 1, a)
                dve.wait_ge(hnhi_ok, ITEMS * g + n + 1)
                less_hi(hn_lo[:, j], t_bank(j), hn_hi[:, j]).then_inc(hnlo_ok, 1)
                update(g, n - 2, b)
                reset(g, n - 1, a)

            def x_unit(g, u):
                nt, bs, _ = unit(u)
                dve.wait_ge(y2_ok, UNITS * g + u + 1)
                ve_.tensor_copy(y2_hi[:, nt, bs], yx[:, 0, nt, bs]).then_inc(y2hi_ok, 1)

            def normed(g, i, stored):
                nt, bs, _ = PARTS[i]
                dve.wait_ge(rstd_ok, NP * g + i + 1)
                if stored:
                    dve.wait_ge(out_ok, GB * g)
                    dve.wait_ge(st_out, 16 * (GB - 1) * g)
                for b in range(bs.start, bs.stop):
                    last = ve_.tensor_scalar(hx[:, nt, b], xw0[:, nt, b], mv[:, nt, b, 0:1],
                                             rstd[:, nt, b:b + 1], ALU.subtract, ALU.mult)
                last.then_inc(hxl_ok, 1)
                dve.wait_ge(hxl_ok, 2 * g + i - NP + 3)
                return (hn_hi[:, bs, nt], hn_lo[:, bs, nt], hx[:, nt, bs])

            def conv_rest(g, between=None):
                def node_lo(nt):
                    dve.wait_ge(hnhi_ok, ITEMS * g + nt + 1)
                    less_hi(hn_lo[:, :, nt], hx[:, nt], hn_hi[:, :, nt]).then_inc(hnlo_ok, 1)

                for nt in range(NT):
                    dve.wait_ge(l1_done, NT * g + nt + 1)
                    ve_.scalar_tensor_tensor(xw1[:, nt], ps[:, L1_BANKS[nt]].rearrange("p (b d) -> p b d", d=P),
                                             ndinv2[:, nt:nt + 1], xw1[:, nt], ALU.mult, ALU.add).then_inc(y1_ok, 1)
                    if between and nt < 2:
                        between(nt + 2)
                dve.wait_ge(y1hi_ok, NT * g + NT)
                less_hi(y1_lo[:, NT - 1], xw1[:, NT - 1], y1_hi[:, NT - 1]).then_inc(y1lo_last, 1)

                def sums(i):
                    nt, bs, bank = PARTS[i]
                    dve.wait_ge(base_ok, NT * g + nt + 1)
                    dve.wait_ge(l2_done, NP * g + i + 1)
                    cols = slice(bs.start * P, bs.stop * P)
                    ve_.scalar_tensor_tensor(xw0[:, nt, bs], ps[:, bank, cols].rearrange("p (b d) -> p b d", d=P),
                                             ndinv[:, nt:nt + 1], xw0[:, nt, bs], ALU.mult, ALU.add).then_inc(x1_ok, 1)
                    dve.wait_ge(x1_ok, NP * g + i + 1)
                    for b in range(bs.start, bs.stop):
                        ve_.bn_stats(st[:, nt, b, :], xw0[:, nt, b, :])
                    dve.drain()
                    for b in range(bs.start, bs.stop):
                        last = ve_.bn_aggr(mv[:, nt, b, :], st[:, nt, b, :])
                    last.then_inc(mv_ok, 1)

                sums(0)
                sums(1)
                sums(2)
                node_lo(0)
                sums(NP - 2)
                node_lo(1)
                hi, lo, h = normed(g, NP - 2, stored=between is not None)
                ve_.tensor_copy(hi, h).then_inc(half_hi, 1)
                dve.wait_ge(half_hi, g + 1)
                less_hi(lo, h, hi).then_inc(half_ok, 1)
                node_lo(2)
                sums(NP - 1)

            def first_state_lo(g, j):
                dve.wait_ge(hThi_ok, SPLITS * g + j + 1)
                less_hi(hT_lo[:, j], hT[:, j], hT_hi[:, j]).then_inc(hTlo_ok, 1)

            def gated(g):
                first_state_lo(g, 0)
                neighbours_lo(g, 0, 0)
                first_state_lo(g, 1)
                hi, lo, h = normed(g, NP - 1, stored=False)
                ve_.tensor_copy(hi, h).then_inc(hnhi_ok, 1)
                dve.wait_ge(hnhi_ok, ITEMS * g + NT)
                less_hi(lo, h, hi).then_inc(hnlo_ok, 1)
                neighbours_lo(g, 1, 1)
                reset(g, 0, 0)
                reset(g, 1, 1)
                difference(g, 0, 0)
                neighbours_lo(g, 2, 2)
                mix(g, 0, 0)
                update(g, 1, 1)
                reset(g, 2, 2)
                with dve.Fori(1, STEPS) as s:
                    for j in range(GB):
                        slot(g, GB * s + j, j)

            def last_sum(g, j):
                dve.wait_ge(t_done, ITEMS * g + ITEMS - GB + j + 1)
                ve_.tensor_tensor(hx[:, :, j, :], t_bank(j), hx[:, :, j, :], ALU.add).then_inc(sum_ok, 1)
                dve.wait_ge(sum_ok, GB * g + j + 1)
                for t in range(NT):
                    ve_.bn_stats(so[:, j, t, :], hx[:, t, j, :])
                dve.drain()
                for t in range(NT):
                    last = ve_.bn_aggr(mo[:, j, t, :], so[:, j, t, :])
                last.then_inc(mo_ok, 1)

            def turn(g):
                neighbours_lo(g, ITEMS - 1, GB - 1)
                update(g, ITEMS - 2, GB - 2)
                reset(g, ITEMS - 1, GB - 1)
                x_unit(g + 1, 0)
                x_unit(g + 1, 1)
                last_sum(g, 0)
                x_unit(g + 1, 2)
                x_unit(g + 1, 3)
                update(g, ITEMS - 1, GB - 1)
                for u in range(4, UNITS):
                    x_unit(g + 1, u)
                last_sum(g, 1)
                conv_rest(g + 1, lambda j: last_sum(g, j))

            def end(g):
                neighbours_lo(g, ITEMS - 1, GB - 1)
                last_sum(g, 0)
                reset(g, ITEMS - 1, GB - 1)
                last_sum(g, 1)
                dve.wait_ge(h_ok, ITEMS * g + ITEMS - 1)
                update(g, ITEMS - 1, GB - 1)
                last_sum(g, 2)
                last_sum(g, 3)
                dve.wait_ge(ro_ok, GB * g + GB)
                dve.wait_ge(st_last, 16 * g)
                for t in range(NT):
                    last = ve_.tensor_scalar(yo[:, t], hx[:, t, GB - 1], mo[:, GB - 1, t, 0:1],
                                             ro[:, GB - 1, t:t + 1], ALU.subtract, ALU.mult)
                last.then_inc(end_ok, 1)

            for u in range(UNITS):
                x_unit(0, u)
            gate_weights()
            conv_rest(0)
            with dve.Fori(0, NG - 1) as g:
                gated(g)
                turn(g)
            gated(NG - 1)
            end(NG - 1)

        @block.tensor
        def _(pe):
            mm = nc.tensor.matmul

            def x_unit(g, u, free=None):
                nt, bs, banks = unit(u)
                if u < 2:
                    pe.wait_ge(xlo_ok, GB * g + 2 * u + 2)
                if free is not None:
                    pe.wait_ge(*free)
                elif u in X_BEFORE:
                    pe.wait_ge(xw_ok, UNITS * g + X_BEFORE[u] + 1)
                w_hi, w_lo = (w[:].rearrange("p k d -> p (k d)") for w in (cat_hi, cat_lo))
                rows = slice(nt * P, (nt + 1) * P)
                for i in range(2):
                    bank, b = banks[:, i, 0:NCHEB * P], bs.start + i
                    mm(bank, xf_hi[:, b, rows], w_hi, start=True, stop=False)
                    mm(bank, xf_hi[:, b, rows], w_lo, start=False, stop=False)
                    last = mm(bank, xf_lo[:, b, rows], w_hi, start=False, stop=True)
                last.then_inc(xw_done, 1)

            def aggregate(bank, nt, hi, lo, bs=slice(0, GB), hi_ready=None, lo_ready=None):
                flat = "p b d -> p (b d)"
                bank = bank[:, bs.start * P:bs.stop * P]
                for kt in range(NT):
                    if hi_ready:
                        hi_ready(kt)
                    for i, a in enumerate(lap(kt, nt)):
                        mm(bank, a, hi[:, kt, bs].rearrange(flat), start=kt == 0 and i == 0, stop=False)
                for kt in range(NT):
                    if lo_ready:
                        lo_ready(kt)
                    last = mm(bank, lap(kt, nt)[0], lo[:, kt, bs].rearrange(flat), start=False, stop=kt == NT - 1)
                return last

            def conv_rest(g, between=None):
                def y2_hi_ready(kt):
                    if kt == 0:
                        pe.wait_ge(xw_ok, UNITS * g + 5)
                    pe.wait_ge(y2hi_ok, UNITS * g + 2 * kt + 2)

                def y2_lo_ready(kt):
                    pe.wait_ge(y2lo_ok, UNITS * g + 2 * kt + 2)

                def y1_hi_ready(kt):
                    pe.wait_ge(y1hi_ok, NT * g + kt + 1)

                def y1_lo_ready(kt):
                    if kt < NT - 1:
                        pe.wait_ge(y1lo_ok, (NT - 1) * g + kt + 1)
                    else:
                        pe.wait_ge(y1lo_last, g + 1)

                for nt in range(NT):
                    waits = (None, None) if nt else (y2_hi_ready, y2_lo_ready)
                    aggregate(ps[:, L1_BANKS[nt]], nt, y2_hi, y2_lo, slice(0, GB), *waits).then_inc(l1_done, 1)
                    if between and nt == 0:
                        between()
                for i, (nt, bs, bank) in enumerate(PARTS):
                    if i == NP - 1:
                        pe.wait_ge(x1_ok, NP * g + NT - 1)
                    waits = (None, None) if i else (y1_hi_ready, y1_lo_ready)
                    aggregate(ps[:, bank], nt, y1_hi, y1_lo, bs, *waits).then_inc(l2_done, 1)

            def weight(w, bank, hi, lo, start, stop):
                mm(bank, gt_hi[:, w], hi, start=start, stop=False)
                mm(bank, gt_lo[:, w], hi, start=False, stop=False)
                return mm(bank, gt_hi[:, w], lo, start=False, stop=stop)

            def neighbours(g, n, j, part):
                bank = ps[:, M_BANK + j % 2]
                runs = [(hn_hi, kt, a) for kt in range(NT) for a in (adj_hi, adj_lo)]
                runs += [(hn_lo, kt, adj_hi) for kt in range(NT)]
                half = len(runs) // 2
                for i in range(part * half, (part + 1) * half):
                    h, kt, a = runs[i]
                    if i == 0:
                        pe.wait_ge(hnhi_ok, ITEMS * g + n + 1)
                    if i == 2 * NT:
                        pe.wait_ge(hnlo_ok, ITEMS * g + n + 1)
                    last = mm(bank, h[:, j, kt, :], a[:, kt], start=i == 0, stop=i == len(runs) - 1)
                if part == 1:
                    last.then_inc(m_done, 1)

            def first_neighbours(j, kt):
                bank = ps[:, M_BANK + j]
                mm(bank, hn_hi[:, j, kt, :], adj_hi[:, kt], start=kt == 0, stop=False)
                mm(bank, hn_hi[:, j, kt, :], adj_lo[:, kt], start=False, stop=False)
                return mm(bank, hn_lo[:, j, kt, :], adj_hi[:, kt], start=False, stop=kt == NT - 2)

            def gates_h(g, n, j):
                pe.wait_ge(hTlo_ok, SPLITS * g + n + 1)
                weight(U3, ps[:, Z_BANK + j % 2], hT_hi[:, j], hT_lo[:, j], True, False)

            def gates_z(g, n, j):
                a = j % 2
                pe.wait_ge(mlo_ok, ITEMS * g + n + 1)
                weight(GZ, ps[:, Z_BANK + a], m_hi[:, a], m_lo[:, a], False, True).then_inc(z_done, 1)

            def gates_r(g, n, j):
                a = j % 2
                bank = ps[:, Z_BANK + a]
                pe.wait_ge(z_ok, ITEMS * g + n + 1)
                for i, (w, m) in enumerate(((gt_hi, m_hi), (gt_lo, m_hi), (gt_hi, m_lo))):
                    last = mm(bank, w[:, GR], m[:, a], start=False, stop=i == 2, skip_group_check=True)
                last.then_inc(r_done, 1)

            def cand_m(g, n, j, reuse=True):
                a = j % 2
                if reuse:
                    pe.wait_ge(v_ok, ITEMS * g + n - 1)
                weight(GV, ps[:, V_BANK + a], m_hi[:, a], m_lo[:, a], True, False)

            def cand_h_hi(g, n, j):
                a = j % 2
                bank = ps[:, V_BANK + a]
                pe.wait_ge(rhhi_ok, ITEMS * g + n + 1)
                mm(bank, gt_hi[:, U5], rh_hi[:, a], start=False, stop=False)
                mm(bank, gt_lo[:, U5], rh_hi[:, a], start=False, stop=False)

            def cand_h_lo(g, n, j):
                a = j % 2
                bank = ps[:, V_BANK + a]
                pe.wait_ge(rhlo_ok, ITEMS * g + n + 1)
                mm(bank, gt_hi[:, U5], rh_lo[:, a], start=False, stop=True).then_inc(v_done, 1)

            def to_node(g, n, j):
                pe.wait_ge(h_ok, ITEMS * g + n + 1)
                for t in range(NT):
                    last = nc.tensor.transpose(ps[:, T_BANK + j % 2, t * P:(t + 1) * P],
                                               hT[:, j, t * P:(t + 1) * P], ident[:])
                last.then_inc(t_done, 1)

            def slot(g, n, j):
                a, b = (j - 1) % GB, (j - 2) % GB
                pe.wait_ge(hnlo_ok, ITEMS * g + n - 1)
                to_node(g, n - GB, j)
                cand_h_hi(g, n - 2, b)
                gates_h(g, n - 1, a)
                cand_h_lo(g, n - 2, b)
                gates_z(g, n - 1, a)
                neighbours(g, n, j, 0)
                gates_r(g, n - 1, a)
                cand_m(g, n - 1, a)
                neighbours(g, n, j, 1)

            def gated(g):
                def transposed(t, js=range(GB)):
                    for j in js:
                        last = nc.tensor.transpose(ps[:, HX_BANKS[j], t * P:(t + 1) * P], hx[:, t, j, :], ident[:])
                        if t == NT - 1:
                            last.then_inc(hxT_done, 1)

                for t in range(2):
                    pe.wait_ge(hx_ok, (NT - 1) * g + t + 1)
                    transposed(t)
                    pe.wait_ge(hnlo_ok, ITEMS * g + t + 1)
                    for j in range(2):
                        first_neighbours(j, t)
                pe.wait_ge(hx_ok, (NT - 1) * g + NT - 1)
                transposed(NT - 2)
                pe.wait_ge(hxl_ok, 2 * g + 1)
                transposed(NT - 1, (0, 1))
                pe.wait_ge(half_ok, g + 1)
                for j in range(2):
                    first_neighbours(j, NT - 1)
                pe.wait_ge(hnlo_ok, ITEMS * g + NT - 1)
                for j in range(2):
                    first_neighbours(j, NT - 2).then_inc(m_done, 1)
                gates_h(g, 0, 0)
                gates_z(g, 0, 0)
                gates_h(g, 1, 1)
                pe.wait_ge(hxl_ok, 2 * g + 2)
                transposed(NT - 1, (2, 3))
                gates_r(g, 0, 0)
                gates_z(g, 1, 1)
                pe.wait_ge(hThi_ok, SPLITS * g + 3)
                cand_m(g, 0, 0, reuse=False)
                pe.wait_ge(hnlo_ok, ITEMS * g + NT)
                neighbours(g, 2, 2, 0)
                gates_r(g, 1, 1)
                cand_h_hi(g, 0, 0)
                cand_h_lo(g, 0, 0)
                cand_m(g, 1, 1, reuse=False)
                neighbours(g, 2, 2, 1)
                gates_h(g, 2, 2)
                cand_h_hi(g, 1, 1)
                cand_h_lo(g, 1, 1)
                gates_z(g, 2, 2)
                neighbours(g, 3, 3, 0)
                gates_r(g, 2, 2)
                cand_m(g, 2, 2)
                neighbours(g, 3, 3, 1)
                with pe.Fori(1, STEPS) as s:
                    for j in range(GB):
                        slot(g, GB * s + j, j)

            def last_to_node(g, i):
                pe.wait_ge(sum_ok, GB * g + i + 1)
                to_node(g, ITEMS - 2 + i, 2 + i)

            def turn(g, follow):
                ends = ITEMS * g + ITEMS
                cand_h_hi(g, ITEMS - 2, GB - 2)
                gates_h(g, ITEMS - 1, GB - 1)
                cand_h_lo(g, ITEMS - 2, GB - 2)
                pe.wait_ge(hnlo_ok, ends)
                to_node(g, ITEMS - 4, 0)
                gates_z(g, ITEMS - 1, GB - 1)
                to_node(g, ITEMS - 3, 1)
                if follow:
                    x_unit(g + 1, 0, free=(mlo_ok, ends))
                gates_r(g, ITEMS - 1, GB - 1)
                cand_m(g, ITEMS - 1, GB - 1)
                if follow:
                    x_unit(g + 1, 1, free=(r_ok, ends))
                    x_unit(g + 1, 2)
                cand_h_hi(g, ITEMS - 1, GB - 1)
                cand_h_lo(g, ITEMS - 1, GB - 1)
                if follow:
                    x_unit(g + 1, 3)
                    x_unit(g + 1, 4, free=(v_ok, ends))
                    for u in range(5, UNITS):
                        x_unit(g + 1, u)
                    last_to_node(g, 0)
                    conv_rest(g + 1, lambda: last_to_node(g, 1))
                else:
                    last_to_node(g, 0)
                    last_to_node(g, 1)

            pe.wait_ge(ones_ok, 1)
            for kt in range(NT):
                for part, (full, block) in enumerate(((adj_hi, dia_hi), (adj_lo, dia_lo))):
                    pe.wait_ge(dia_ok, 2 * kt + part + 1)
                    for nt in range(NT):
                        a = block[:, kt] if kt == nt else full[:, kt, nt * P:(nt + 1) * P]
                        last = mm(ps[0:2, nt, 0:P], ones_r[:], a, start=kt == 0 and part == 0,
                                  stop=kt == NT - 1 and part == 1)
            last.then_inc(row_done, 1)
            pe.wait_ge(row_ok, 1)
            for nt in range(NT):
                last = nc.tensor.transpose(ps[:, 0, 2 * nt:2 * nt + 2], deg_row[:, nt * P:(nt + 1) * P],
                                           ident[0:2, 0:2])
            last.then_inc(deg_ok, 1)
            pe.wait_ge(cat_ok, 1)
            for u in range(UNITS):
                x_unit(0, u)
            conv_rest(0)
            with pe.Fori(0, NG - 1) as g:
                gated(g)
                turn(g, True)
            gated(NG - 1)
            turn(NG - 1, False)


def kernel(**inputs):
    import numpy as np
    import concourse.bacc as bacc
    from concourse.bass_utils import run_bass_kernel_spmd

    def arr(name):
        return np.asarray(inputs[name])

    P = 128
    x = arr("x")
    xT = np.ascontiguousarray(x.transpose(0, 2, 1))
    adjT = np.ascontiguousarray(arr("adj").T)
    cheb_w = np.ascontiguousarray(arr("L0_gnn_Ws").transpose(1, 0, 2))
    gate_w = np.ascontiguousarray(np.stack([arr(f"L1_gnn_w{k}_w").T.reshape(2, P, P) for k in (3, 4, 5)])
                                  .transpose(2, 0, 1, 3))
    gate_u = np.ascontiguousarray(np.stack([arr(f"L1_gnn_u{k}_w").T for k in (3, 5)]).transpose(1, 0, 2))
    gate_b = np.ascontiguousarray(np.stack([arr(f"L1_gnn_{k}_b") for k in ("w3", "w4", "w5", "u3", "u5")]).T)
    cheb_b = arr("L0_gnn_bias")
    arrays = {"xT": xT, "adjT": adjT, "cheb_w": cheb_w, "gate_w": gate_w, "gate_u": gate_u,
              "gate_b": gate_b, "cheb_b": cheb_b}

    nc = bacc.Bacc("TRN2", target_bir_lowering=False, num_devices=1)
    args = [nc.dram_tensor(f"in_{n}", a.shape, mybir.dt.from_np(a.dtype), kind="ExternalInput").ap()
            for n, a in arrays.items()]
    out = nc.dram_tensor("out_0", x.shape, mybir.dt.float32, kind="ExternalOutput").ap()
    cheb_gated_graph_kernel(nc, *args, out)
    r = run_bass_kernel_spmd(nc, [{f"in_{n}": a for n, a in arrays.items()}], core_ids=[0])
    return r.results[0]["out_0"]
```
